# Optimizing a Trainium2 kernel written in Bass

```python
import numpy as np
import jax
import jax.numpy as jnp

def _softmax(x, axis=-1):
    return jax.nn.softmax(x, axis=axis)

def _gelu(x):
    return jax.nn.gelu(x, approximate=True)

def _silu(x):
    return jax.nn.silu(x)

def _sigmoid(x):
    return jax.nn.sigmoid(x)

def _layernorm(x, axis=-1, eps=1e-05):
    m = jnp.mean(x, axis=axis, keepdims=True)
    v = jnp.var(x, axis=axis, keepdims=True)
    return (x - m) / jnp.sqrt(v + eps)

def _scatter_add(tgt, idx, src, axis=0):
    return tgt.at[idx].add(src)

def _segment_sum(src, seg, n):
    return jax.ops.segment_sum(src, seg, n)
kernel_name = 'mk_macaron_d1_jaxref_r8_ea3c8a'

def setup_inputs(seed: int=0):
    np.random.seed(seed)
    _w = jnp.asarray

    def _L0_attn_setup():
        import jax, jax.numpy as jnp
        import numpy as np
        B, S, D_MODEL = (2, 256, 128)
        NUM_HEADS, ATTN_DIM = (16, 64)
        key = jax.random.key(seed)
        ks = jax.random.split(key, 9)
        scale = 1.0 / np.sqrt(D_MODEL)
        states = jax.random.normal(ks[0], (B, S, D_MODEL), dtype=jnp.float32)
        Wq = jax.random.normal(ks[1], (D_MODEL, NUM_HEADS * ATTN_DIM), dtype=jnp.float32) * scale
        bq = jnp.zeros((NUM_HEADS * ATTN_DIM,), dtype=jnp.float32)
        Wk = jax.random.normal(ks[2], (D_MODEL, NUM_HEADS * ATTN_DIM), dtype=jnp.float32) * scale
        bk = jnp.zeros((NUM_HEADS * ATTN_DIM,), dtype=jnp.float32)
        Wv = jax.random.normal(ks[3], (D_MODEL, NUM_HEADS * ATTN_DIM), dtype=jnp.float32) * scale
        bv = jnp.zeros((NUM_HEADS * ATTN_DIM,), dtype=jnp.float32)
        Wo = jax.random.normal(ks[4], (NUM_HEADS * ATTN_DIM, D_MODEL), dtype=jnp.float32) * scale
        bo = jnp.zeros((D_MODEL,), dtype=jnp.float32)
        return {'states': states, 'Wq': Wq, 'bq': bq, 'Wk': Wk, 'bk': bk, 'Wv': Wv, 'bv': bv, 'Wo': Wo, 'bo': bo}
    _L0_attn_in = _L0_attn_setup()

    def _L0_ffn_setup():
        import jax, jax.numpy as jnp
        import numpy as np
        B, S, D = (4, 256, 128)
        E = 8
        DFF = 512
        CAP_FACTOR = 1.25
        key = jax.random.key(seed)
        ks = jax.random.split(key, 4)
        std_gate = float(np.sqrt(0.1 / D))
        inputs = jax.random.normal(ks[0], (B, S, D), dtype=jnp.float32)
        gate_w = jax.random.normal(ks[1], (E, D), dtype=jnp.float32) * std_gate
        w1 = jax.random.normal(ks[2], (E, D, DFF), dtype=jnp.float32) * (1.0 / np.sqrt(D))
        b1 = jnp.zeros((E, DFF), dtype=jnp.float32)
        w2 = jax.random.normal(ks[3], (E, DFF, D), dtype=jnp.float32) * (1.0 / np.sqrt(DFF))
        b2 = jnp.zeros((E, D), dtype=jnp.float32)
        return {'inputs': inputs, 'gate_w': gate_w, 'w1': w1, 'b1': b1, 'w2': w2, 'b2': b2}
    _L0_ffn_in = _L0_ffn_setup()
    _d = {'L0_attn_states': _L0_attn_in['states'], 'L0_attn_Wq': _L0_attn_in['Wq'], 'L0_attn_bq': _L0_attn_in['bq'], 'L0_attn_Wk': _L0_attn_in['Wk'], 'L0_attn_bk': _L0_attn_in['bk'], 'L0_attn_Wv': _L0_attn_in['Wv'], 'L0_attn_bv': _L0_attn_in['bv'], 'L0_attn_Wo': _L0_attn_in['Wo'], 'L0_attn_bo': _L0_attn_in['bo'], 'L0_ffn_gate_w': _L0_ffn_in['gate_w'], 'L0_ffn_w1': _L0_ffn_in['w1'], 'L0_ffn_b1': _L0_ffn_in['b1'], 'L0_ffn_w2': _L0_ffn_in['w2'], 'L0_ffn_b2': _L0_ffn_in['b2']}
    _x0 = _d['L0_attn_states']
    _d['L0_attn_states'] = jax.random.normal(jax.random.fold_in(jax.random.key(seed), 1), (4, 512, 128), dtype=_x0.dtype)
    del _x0
    return _d

def reference(L0_attn_states, L0_attn_Wq, L0_attn_bq, L0_attn_Wk, L0_attn_bk, L0_attn_Wv, L0_attn_bv, L0_attn_Wo, L0_attn_bo, L0_ffn_gate_w, L0_ffn_w1, L0_ffn_b1, L0_ffn_w2, L0_ffn_b2):

    def _L0_attn_ref(states, Wq, bq, Wk, bk, Wv, bv, Wo, bo):
        import jax, jax.numpy as jnp
        import numpy as np
        B, S, D_MODEL = (2, 256, 128)
        NUM_HEADS, ATTN_DIM = (16, 64)
        b, s, _ = states.shape
        h, d = (NUM_HEADS, ATTN_DIM)

        def proj(W, bias):
            y = jnp.tanh(states @ W + bias)
            return y.reshape(b, s, h, d).transpose(0, 2, 1, 3)
        q, k, v = (proj(Wq, bq), proj(Wk, bk), proj(Wv, bv))
        alpha = jnp.einsum('bhqd,bhkd->bhqk', q, k) / jnp.sqrt(jnp.float32(d))
        causal = jnp.tril(jnp.ones((s, s), dtype=bool))
        alpha = jnp.where(causal, alpha, jnp.finfo(jnp.float32).min)
        alpha = jax.nn.softmax(alpha, axis=-1)
        ctx = jnp.einsum('bhqk,bhkd->bhqd', alpha, v)
        ctx = ctx.transpose(0, 2, 1, 3).reshape(b, s, h * d)
        return jnp.tanh(ctx @ Wo + bo)

    def _L0_ffn_ref(inputs, gate_w, w1, b1, w2, b2):
        import jax, jax.numpy as jnp
        import numpy as np
        B, S, D = (4, 256, 128)
        E = 8
        DFF = 512
        CAP_FACTOR = 1.25
        d_model = inputs.shape[-1]
        tokens = inputs.reshape(-1, d_model)
        T = tokens.shape[0]
        num_experts = gate_w.shape[0]
        capacity = int(np.ceil(CAP_FACTOR * T / num_experts))
        logits = jnp.einsum('td,ed->te', tokens.astype(jnp.float32), gate_w)
        probs = jax.nn.softmax(logits, axis=-1)
        expert_idx = jnp.argmax(probs, axis=-1)
        mask = jax.nn.one_hot(expert_idx, num_experts, dtype=jnp.float32)
        ranks = jnp.cumsum(mask, axis=0) - 1.0
        keep = (ranks < capacity) * mask
        pos = ranks.astype(jnp.int32)
        sec_mask = jax.nn.one_hot(pos, capacity, dtype=jnp.float32) * keep[:, :, None]
        combine_weights = probs[:, :, None] * sec_mask
        dispatch = jnp.einsum('tec,td->ecd', sec_mask, tokens)
        h = jax.nn.relu(jnp.einsum('ecd,edh->ech', dispatch, w1) + b1[:, None, :])
        expert_out = jnp.einsum('ech,ehd->ecd', h, w2) + b2[:, None, :]
        ans = jnp.einsum('tec,ecd->td', combine_weights, expert_out)
        return ans.reshape(inputs.shape)
    x = L0_attn_states
    x = x + 0.5 * _L0_ffn_ref(_layernorm(x, axis=-1), L0_ffn_gate_w, L0_ffn_w1, L0_ffn_b1, L0_ffn_w2, L0_ffn_b2)
    x = x + _L0_attn_ref(_layernorm(x, axis=-1), L0_attn_Wq, L0_attn_bq, L0_attn_Wk, L0_attn_bk, L0_attn_Wv, L0_attn_bv, L0_attn_Wo, L0_attn_bo)
    x = x + 0.5 * _L0_ffn_ref(_layernorm(x, axis=-1), L0_ffn_gate_w, L0_ffn_w1, L0_ffn_b1, L0_ffn_w2, L0_ffn_b2)
    return x

_drawn_inputs = setup_inputs


def setup_inputs(seed=0):
    import zlib

    import numpy as np

    out = dict(_drawn_inputs(seed))
    spreads = {'L0_attn_bq': (0.0, 0.685),
     'L0_attn_bk': (0.0, 0.8),
     'L0_attn_bv': (0.0, 0.1),
     'L0_attn_bo': (0.0, 0.1),
     'L0_ffn_b1': (0.0, 0.509),
     'L0_ffn_b2': (0.0, 0.385)}
    factors = {}
    for name, (base, spread) in spreads.items():
        noise = np.random.default_rng([zlib.crc32(name.encode()), seed]).standard_normal(out[name].shape)
        drawn = base * np.exp(spread * noise) if base else spread * noise
        out[name] = jnp.asarray(drawn.astype(out[name].dtype))
    for name, factor in factors.items():
        out[name] = (out[name] * factor).astype(out[name].dtype)
    return out
```

```python
from contextlib import ExitStack

import numpy as np

import concourse.bass as bass
from concourse import mybir

F32 = mybir.dt.float32
F16 = mybir.dt.float16
BF16 = mybir.dt.bfloat16
U32 = mybir.dt.uint32
ALU = mybir.AluOpType
ACT = mybir.ActivationFunctionType
X_AXIS = mybir.AxisListType.X
ABSMAX = bass.bass_isa.ReduceOp.max

P = 128
NT = 16
GT = 4
NG = NT // GT
GN = GT * P
E = 8
CAP = 320
SLOTS = E * CAP
DFF = 512
FT = DFF // P
NPAIR = 8
HD = 64
EPS = 1e-5
NEG = -30000.0
LN_PSHIFT = float(np.log(16.0))
LN_STEPS = 5
ROUTE_STEPS = 14
KOFF = [0, 512, 1024, 896]
CHUNKS = [(0, 512, [0]), (512, 512, [1, 3]), (1024, 256, [2])]
POOL_CHUNKS = [0]
V_CHUNKS = [1, 2]
B1_COL, BQ_COL, BK_COL, BO_COL, GW_COL, ROWS = 0, 32, 40, 48, 49, 57


class Steps:

    def __init__(self, eng, sem, base, total):
        self.eng, self.sem, self.base, self.total, self.k = eng, sem, base, total, 0

    def done(self, ins):
        self.k += 1
        ins.then_inc(self.sem, 1)
        self.eng.wait_ge(self.sem, self.base + self.k)

    def end(self):
        assert self.k == self.total, (self.k, self.total)


def macaron(nc, x_d, wq, bq, wk, bk, wv, bv, wo, bo, gate_w, w1, b1, w2, b2, out):
    ctx = ExitStack()
    with ctx:
        def sb(name, shape, dt):
            return ctx.enter_context(nc.sbuf_tensor(name, shape, dt))

        def bank(name):
            return ctx.enter_context(nc.psum_tensor(name, [P, 512], F32))

        def sem(name):
            return ctx.enter_context(nc.semaphore(name))

        disp = nc.dram_tensor("disp_scratch", [SLOTS + NT * P, P], F32, kind="Internal").ap()
        ydram = nc.dram_tensor("y_scratch", [SLOTS, P], F32, kind="Internal").ap()
        x_v = x_d.rearrange("b s d -> (b s) d").rearrange("(t p) d -> p t d", p=P)
        out_v = out.rearrange("b s d -> (b s) d").rearrange("(t p) d -> p t d", p=P)

        X = sb("X", [P, NT, P], F32)
        XN = sb("XN", [P, NT, P], F32)
        xn = sb("xn", [P, GT, P], F32)
        G = sb("G", [P, NT, P], F32)
        xT = sb("xT", [P, GN], F32)
        XH = sb("XH", [P, NT * P], F16)
        XL = sb("XL", [P, NT * P], F16)
        Wf = sb("Wf", [P, 4096], F32)
        WH = sb("WH", [P, 4096], F16)
        WL = sb("WL", [P, 4096], F16)
        bvf = sb("bvf", [P, 1024], F32)
        bvr = sb("bvr", [P, 1024], F32)
        bvt = sb("bvt", [P, 1024], BF16)
        bvu = sb("bvu", [P, 1024], BF16)
        bvs = sb("bvs", [P, 1024], BF16)
        b2bc = sb("b2bc", [P, E * P], F32)
        rows = sb("rows", [ROWS, P], F32)
        RT = sb("RT", [P, ROWS], F32)
        zero = sb("zero", [P, SLOTS // 2], F32)
        identf = sb("identf", [P, P], F32)
        identb = sb("identb", [P, P], BF16)
        onesb = sb("onesb", [P, P], BF16)
        lower = sb("lower", [P, P], BF16)
        maskn = sb("maskn", [P, P], BF16)
        pick = sb("pick", [P, E], F32)
        ebase = sb("ebase", [P, E], F32)
        tok = sb("tok", [P, NT], F32)
        mhalf = sb("mhalf", [P, GT], F32)
        pshift = sb("pshift", [P, 1], F32)
        spare = sb("spare", [P, 1], F32)
        st = sb("st", [P, GT, 6], F32)
        mv = sb("mv", [P, GT, 2], F32)
        ve = sb("ve", [P, GT], F32)
        r0 = sb("r0", [P, GT], F32)
        ra = sb("ra", [P, GT], F32)
        rb = sb("rb", [P, GT], F32)
        rstd = sb("rstd", [P, GT], F32)
        mx = sb("mx", [P, GT], F32)
        dl = sb("dl", [P, GT, E], F32)
        el = sb("el", [P, GT, E], F32)
        m0 = sb("m0", [P, GT, E], F32)
        ms = sb("ms", [P, GT, E], F32)
        m2 = sb("m2", [P, GT], F32)
        mask = sb("mask", [P, GT, E], BF16)
        se = sb("se", [P, GT], F32)
        pr = sb("pr", [P, GT], F32)
        pos = sb("pos", [P, GT, E], F32)
        AB = sb("AB", [P, 2, GT, E], F32)
        rs = sb("rs", [P, 2, GT], F32)
        keep = sb("keep", [P, GT], F32)
        slot = sb("slot", [P, GT], F32)
        sd = sb("sd", [P, GT], F32)
        sk = sb("sk", [P, GT], F32)
        carry = sb("carry", [P, E], F32)
        wts = sb("wts", [P, NT], F32)
        idx_s = sb("idx_s", [P, NT], U32)
        idx_g = sb("idx_g", [P, NT], U32)
        XE = [sb(f"XE{u}", [P, 3, P], F32) for u in range(2)]
        W1 = [sb(f"W1_{u}", [P, DFF], F32) for u in range(2)]
        W2 = [sb(f"W2_{u}", [P, FT, P], F32) for u in range(2)]
        xeT = sb("xeT", [P, CAP], F32)
        hT = sb("hT", [P, FT, CAP], F32)
        Y = [sb(f"Y{u}", [P, 3, P], F32) for u in range(2)]
        am = sb("am", [P, 8], F32)
        Tq = sb("Tq", [P, GN], F32)
        Tk = sb("Tk", [P, GN], F32)
        Tv = sb("Tv", [P, GN], F32)
        Qn = sb("Qn", [P, 2, GN], F16)
        Kn = sb("Kn", [P, 2, GN], F16)
        KP = [sb(f"KP{h}", [P, 2, GN], F16) for h in range(2)]
        Vh = sb("Vh", [P, GT, 2, HD + 1], F16)
        Vl = sb("Vl", [P, GT, 2, HD], F16)
        Pf = [sb(f"Pf{h}", [P, 1280], F32) for h in range(2)]
        Ph = [sb(f"Ph{h}", [P, 1280], F16) for h in range(2)]
        Pl = [sb(f"Pl{h}", [P, 1280], F16) for h in range(2)]
        rden = [sb(f"rden{h}", [P, GT], F32) for h in range(2)]
        cn = sb("cn", [P, GT, P], F32)
        CT = sb("CT", [P, NPAIR, 2, GN], F16)
        yT = sb("yT", [P, GN], F32)

        sc = [bank(f"sc{i}") for i in range(3)]
        pj0, pj1, cA, cB, tT = bank("pj0"), bank("pj1"), bank("cA"), bank("cB"), bank("tT")
        cx = [cA, cB]
        hbank = [sc[0], sc[1], sc[2], cA]

        names = """x_in w_in rows_in b2_in bv_in zero_filled consts ks_init bv_zero pool_const
            rt_ps rt_ready carry0 carry_set ln_step var_ready rs_pow xn_ready xn_kept xt_ps xt_ready
            logit_ps dl_ready el_ready mask_ready rank_ps route_step idx_ready scattered
            we_in0 we_in1 xe_in0 xe_in1 xe_ps xe_ready h_ps h_ready y_ps y_ready y_st0 y_st1
            combined amax amax_all wscale bv_ready w_split
            q_ps k_ps v_ps tq tk tv q_hi k_hi v_hi q_lo k_lo v_lo k_pad
            s_ps exp_done p_hi p_lo_v p_lo_p ctx_ps rden_ready ctxn ct_ps ct_hi ct_lo wo_ps yt yt_ps x_added
            x_hi x_lo out_done w_ready""".split()
        S = {n: sem(n) for n in names}
        we_in, xe_in, y_st = [S["we_in0"], S["we_in1"]], [S["xe_in0"], S["xe_in1"]], [S["y_st0"], S["y_st1"]]
        gsem = [sem(f"gathered{g}") for g in range(NG)]
        CREDITED = {"sync": [y_st[0], y_st[1]], "tensor": [S["xt_ps"]], "scalar": [S["xn_kept"], S["yt"]],
                    "vector": [S["x_added"], S["ct_lo"]]}
        block = ctx.enter_context(nc.Block())

        @block.sync
        def _(sp):
            for s in CREDITED["sync"]:
                sp.sem_inc(s, 1)

            def load_weights(e, u):
                sp.dma_start(W1[u][:], w1[bass.ds(e, 1), :, :].rearrange("a d f -> (a d) f")).then_inc(we_in[u], 16)
                sp.dma_start(W2[u][:], w2[bass.ds(e, 1), :, :].rearrange("a (t p) d -> p (a t) d", p=P)).then_inc(we_in[u], 16)

            def load_tokens(e, u):
                sp.dma_start(XE[u][:, 0:2, :], disp[bass.ds(e * CAP, 2 * P), :].rearrange("(p j) d -> p j d", j=2)).then_inc(xe_in[u], 16)
                sp.dma_start(XE[u][0:CAP - 2 * P, 2, :], disp[bass.ds(e * CAP + 2 * P, CAP - 2 * P), :]).then_inc(xe_in[u], 16)

            def store_y(e, u):
                sp.dma_start(ydram[bass.ds(e * CAP, 2 * P), :].rearrange("(p j) d -> p j d", j=2), Y[u][:, 0:2, :]).then_inc(y_st[u], 16)
                sp.dma_start(ydram[bass.ds(e * CAP + 2 * P, CAP - 2 * P), :], Y[u][0:CAP - 2 * P, 2, :]).then_inc(y_st[u], 16)

            sp.dma_start(X[:, :, :], x_v).then_inc(S["x_in"], 16)
            for phase in range(2):
                if phase:
                    sp.wait_ge(S["y_ps"], E)
                load_weights(0, 0)
                load_weights(1, 1)
                sp.wait_ge(S["scattered"], 16 * NT * (phase + 1))
                load_tokens(0, 0)
                load_tokens(1, 1)
                with sp.Fori(0, E // 2 - 1) as ee:
                    for u in range(2):
                        n = E * phase + 2 * ee + u
                        sp.wait_ge(S["y_ps"], n + 1)
                        load_weights(2 * ee + u + 2, u)
                        load_tokens(2 * ee + u + 2, u)
                        sp.wait_ge(S["y_ready"], n + 1)
                        store_y(2 * ee + u, u)
                for u in range(2):
                    sp.wait_ge(S["y_ready"], E * phase + E - 1 + u)
                    store_y(E - 2 + u, u)
            with sp.Fori(0, NG) as g:
                sp.wait_ge(S["combined"], NG + 1 + g)
                sp.dma_start(out_v[:, bass.ds(GT * g, GT), :], X[:, bass.ds(GT * g, GT), :]).then_inc(S["out_done"], 16)
            sp.wait_ge(S["out_done"], 16 * NG)

        @block.gpsimd
        def _(pool):
            pool.memset(identf[:], 0.0).then_inc(S["pool_const"], 1)
            pool.memset(identb[:], 0.0).then_inc(S["pool_const"], 1)
            pool.memset(onesb[:], 1.0).then_inc(S["pool_const"], 1)
            pool.memset(maskn[:], 0.0).then_inc(S["pool_const"], 1)
            pool.memset(lower[:], 1.0).then_inc(S["pool_const"], 1)
            pool.wait_ge(S["pool_const"], 5)
            for m in (identf, identb):
                pool.affine_select(out=m[:], in_=m[:], compare_op=ALU.not_equal, fill=1.0, base=0,
                                   pattern=[[-1, P]], channel_multiplier=1)
            pool.affine_select(out=maskn[:], in_=maskn[:], compare_op=ALU.is_ge, fill=NEG, base=0,
                               pattern=[[1, P]], channel_multiplier=-1)
            pool.affine_select(out=lower[:], in_=lower[:], compare_op=ALU.is_ge, fill=0.0, base=0,
                               pattern=[[1, P]], channel_multiplier=-1)
            pool.iota(pick[:], [[-1, E]], base=E, channel_multiplier=0, allow_small_or_imprecise_dtypes=True)
            pool.iota(ebase[:], [[CAP, E]], base=-1, channel_multiplier=0, allow_small_or_imprecise_dtypes=True)
            pool.iota(tok[:], [[P, NT]], base=SLOTS, channel_multiplier=1, allow_small_or_imprecise_dtypes=True)
            pool.memset(pshift[:], LN_PSHIFT)
            pool.memset(mhalf[:], -0.5).then_inc(S["consts"], 1)
            pool.memset(zero[:], 0.0).then_inc(S["consts"], 1)
            pool.memset(Vh[:, :, :, HD:HD + 1], 1.0)
            pool.memset(bvs[:], 0.0).then_inc(S["ks_init"], 1)
            pool.memset(bvf[:], 0.0).then_inc(S["bv_zero"], 1)

            def inv_std(n):
                pool.wait_ge(S["var_ready"], n + 1)
                pool.tensor_tensor(r0[:], ve[:], mhalf[:], ALU.pow).then_inc(S["rs_pow"], 1)

            def dispatch(phase):
                for g in range(NG):
                    inv_std(8 * phase + g)
                    pool.wait_ge(S["idx_ready"], NG * phase + g + 1)
                    pool.wait_ge(S["xn_kept"], NG * phase + g + 2)
                    if phase == 0 and g == 0:
                        pool.wait_ge(S["zero_filled"], 32)
                    for t in range(GT * g, GT * g + GT):
                        pool.indirect_dma_start(disp, bass.IndirectOffsetOnAxis(ap=idx_s[:, t:t + 1], axis=0),
                                                XN[:, t, :], None).then_inc(S["scattered"], 16)

            def gather(phase, with_norm):
                pool.wait_ge(y_st[0], 16 * E * (phase + 1) + 1)
                pool.wait_ge(y_st[1], 16 * E * (phase + 1) + 1)
                for g in range(NG):
                    for t in range(GT * g, GT * g + GT):
                        pool.indirect_dma_start(G[:, t, :], None, ydram,
                                                bass.IndirectOffsetOnAxis(ap=idx_g[:, t:t + 1], axis=0)
                                                ).then_inc(gsem[g], 16)
                    if with_norm and g:
                        inv_std(NG + g - 1)
                if with_norm:
                    inv_std(2 * NG - 1)

            dispatch(0)
            pool.wait_ge(S["amax"], 1)
            pool.partition_all_reduce(am[:, 1:2], am[:, 0:1], P, ABSMAX).then_inc(S["amax_all"], 1)
            gather(0, True)

            def low(dst, src, hi, done):
                pool.tensor_tensor(dst, src, hi, ALU.subtract).then_inc(done, 1)

            def qk_low(f):
                pool.wait_ge(S["q_hi"], f + 1)
                low(Qn[:, 1, :], Tq[:], Qn[:, 0, :], S["q_lo"])
                pool.wait_ge(S["k_hi"], f + 1)
                low(Kn[:, 1, :], Tk[:], Kn[:, 0, :], S["k_lo"])

            def v_low(f):
                pool.wait_ge(S["v_hi"], f + 1)
                low(Vl[:], Tv[:].rearrange("p (t h d) -> p t h d", t=GT, h=2), Vh[:, :, :, 0:HD], S["v_lo"])

            def step(i, nxt):
                for h in range(2):
                    for c in POOL_CHUNKS:
                        a, n, _ = CHUNKS[c]
                        pool.wait_ge(S["p_hi"], 6 * i + 3 * h + c + 1)
                        low(Pl[h][:, a:a + n], Pf[h][:, a:a + n], Ph[h][:, a:a + n], S["p_lo_p"])
                if nxt:
                    qk_low(i + 1)
                    v_low(i + 1)

            def batch(b, last):
                with pool.Fori(0, NPAIR - 1) as j:
                    step(NPAIR * b + j, True)
                step(NPAIR * b + NPAIR - 1, not last)

            qk_low(0)
            v_low(0)
            with pool.Fori(0, NG - 1) as b:
                batch(b, False)
            batch(NG - 1, True)
            dispatch(1)
            gather(1, False)

        @block.scalar
        def _(act):
            for s in CREDITED["scalar"]:
                act.sem_inc(s, 1)
            act.dma_start(rows[B1_COL:B1_COL + 32, :], b1.rearrange("e (t p) -> (e t) p", p=P)).then_inc(S["rows_in"], 16)
            act.dma_start(rows[BQ_COL:BQ_COL + 8, :], bq.rearrange("(r p) -> r p", p=P)).then_inc(S["rows_in"], 16)
            act.dma_start(rows[BK_COL:BK_COL + 8, :], bk.rearrange("(r p) -> r p", p=P)).then_inc(S["rows_in"], 16)
            act.dma_start(rows[BO_COL:BO_COL + 1, :], bo.rearrange("(r p) -> r p", p=P)).then_inc(S["rows_in"], 16)
            act.dma_start(rows[GW_COL:GW_COL + 8, :], gate_w).then_inc(S["rows_in"], 16)
            act.wait_ge(S["consts"], 2)
            for half in range(2):
                act.dma_start(disp[half * SLOTS // 2:(half + 1) * SLOTS // 2, :].rearrange("(p r) d -> p (r d)", p=P),
                              zero[:]).then_inc(S["zero_filled"], 16)
            for k, w in enumerate((wq, wk, wv)):
                act.dma_start(Wf[:, 1024 * k:1024 * (k + 1)], w).then_inc(S["w_in"], 16)
            act.dma_start(Wf[:, 3072:4096].rearrange("p (r d) -> p r d", d=P), wo.rearrange("(r p) d -> p r d", p=P)).then_inc(S["w_in"], 16)
            act.dma_start(b2bc[:], b2.rearrange("e d -> (e d)").partition_broadcast(P)).then_inc(S["b2_in"], 16)
            act.wait_ge(S["bv_zero"], 1)
            for k in range(3):
                act.dma_start(bvf[32 * k:32 * k + 1, :], bv.rearrange("(a n) -> a n", a=1)).then_inc(S["bv_in"], 16)

            act.wait_ge(S["rt_ps"], 1)
            act.activation(RT[:], pj0[:, 0:ROWS], ACT.Copy).then_inc(S["rt_ready"], 1)

            def route(phase):
                with act.Fori(0, NG) as g:
                    n = NG * phase + g
                    act.wait_ge(S["xn_ready"], 8 * phase + g + 1)
                    act.activation(XN[:, bass.ds(GT * g, GT), :], xn[:], ACT.Copy).then_inc(S["xn_kept"], 1)
                    act.wait_ge(S["xt_ps"], 8 * phase + g + 2)
                    act.activation(xT[:], tT[:], ACT.Copy).then_inc(S["xt_ready"], 1)
                    act.wait_ge(S["dl_ready"], n + 1)
                    act.activation(el[:], dl[:], ACT.Exp).then_inc(S["el_ready"], 1)

            def experts(phase):
                with act.Fori(0, E) as e:
                    for ft in range(FT):
                        act.wait_ge(S["h_ps"], FT * (E * phase + e) + ft + 1)
                        act.activation(hT[:, ft, :], hbank[ft][:, 0:CAP], ACT.Relu,
                                       bias=RT[:, bass.ds(B1_COL + FT * e + ft, 1)]).then_inc(S["h_ready"], 1)

            route(0)
            experts(0)
            with act.Fori(0, NG) as g:
                act.wait_ge(S["xt_ps"], NG + g + 2)
                act.activation(XH[:, bass.ds(GN * g, GN)], tT[:], ACT.Copy).then_inc(S["x_hi"], 1)

            unscale = am[:, 5:6]

            def tanh_qk(f, r):
                act.wait_ge(S["q_ps"], f + 1)
                if not isinstance(f, int):
                    act.wait_ge(S["q_lo"], f)
                act.activation(Tq[:], pj0[:], ACT.Tanh, bias=RT[:, bass.ds(BQ_COL + r, 1)], scale=unscale).then_inc(S["tq"], 1)
                act.wait_ge(S["k_ps"], f + 1)
                if not isinstance(f, int):
                    act.wait_ge(S["k_lo"], f)
                act.activation(Tk[:], pj1[:], ACT.Tanh, bias=RT[:, bass.ds(BK_COL + r, 1)], scale=unscale).then_inc(S["tk"], 1)

            def tanh_v(f):
                act.wait_ge(S["v_ps"], f + 1)
                if not isinstance(f, int):
                    act.wait_ge(S["v_lo"], f)
                act.activation(Tv[:], pj0[:], ACT.Tanh, scale=unscale).then_inc(S["tv"], 1)

            def step(i, r, nxt):
                for h in range(2):
                    for c, (a, n, _) in enumerate(CHUNKS):
                        act.wait_ge(S["s_ps"], 6 * i + 3 * h + c + 1)
                        act.activation(Pf[h][:, a:a + n], sc[c][:, 0:n], ACT.Exp, scale=0.125,
                                       bias=pshift[:]).then_inc(S["exp_done"], 1)
                if nxt is not None:
                    tanh_qk(i + 1, nxt)
                    tanh_v(i + 1)
                act.wait_ge(S["ct_ps"], i + 1)
                act.activation(CT[:, bass.ds(r, 1), 0, :], tT[:], ACT.Copy).then_inc(S["ct_hi"], 1)

            def batch(b, last):
                with act.Fori(0, NPAIR - 1) as j:
                    step(NPAIR * b + j, j, j + 1)
                step(NPAIR * b + NPAIR - 1, NPAIR - 1, None if last else 0)
                act.wait_ge(S["wo_ps"], b + 1)
                act.activation(yT[:], pj1[:], ACT.Tanh, bias=RT[:, BO_COL:BO_COL + 1], scale=unscale).then_inc(S["yt"], 1)

            tanh_qk(0, 0)
            tanh_v(0)
            with act.Fori(0, NG - 1) as b:
                batch(b, False)
            batch(NG - 1, True)
            route(1)
            experts(1)

        @block.tensor
        def _(pe):
            mm = nc.tensor.matmul
            for s in CREDITED["tensor"]:
                pe.sem_inc(s, 1)

            def transpose_group(n):
                pe.wait_ge(S["xn_ready"], n + 1)
                for t in range(GT):
                    last = nc.tensor.transpose(tT[:, P * t:P * t + P], xn[:, t, :], identf[:])
                last.then_inc(S["xt_ps"], 1)

            def route(phase):
                with pe.Fori(0, NG) as g:
                    n = NG * phase + g
                    transpose_group(8 * phase + g)
                    pe.wait_ge(S["xt_ready"], n + 1)
                    for t in range(GT):
                        last = mm(pj0[:, E * t:E * t + E], xT[:, P * t:P * t + P], RT[:, GW_COL:GW_COL + E],
                                  start=True, stop=True)
                    last.then_inc(S["logit_ps"], 1)
                    pe.wait_ge(S["mask_ready"], n + 1)
                    mm(pj1[:, 0:GT * E], lower[:], mask[:].rearrange("p t e -> p (t e)"), start=True, stop=False)
                    for t in range(GT - 1):
                        mm(pj1[:, E * (t + 1):GT * E].rearrange("p (t e) -> p t e", e=E), onesb[:],
                           mask[:, t:t + 1, :].broadcast_to([P, GT - 1 - t, E]), start=False, stop=t == GT - 2)
                    for t in range(GT):
                        last = mm(pj1[:, 64:64 + E], onesb[:], mask[:, t, :], start=t == 0, stop=t == GT - 1)
                    last.then_inc(S["rank_ps"], 1)

            def experts(phase):
                def tokens(n, u, cnt):
                    pe.wait_ge(xe_in[u], 32 * (cnt + 1))
                    nc.tensor.transpose(tT[:, 0:P], XE[u][:, 0, :], identf[:])
                    nc.tensor.transpose(tT[:, P:2 * P], XE[u][:, 1, :], identf[:])
                    m = CAP - 2 * P
                    nc.tensor.transpose(tT[:, 2 * P:CAP], XE[u][0:m, 2, :], identf[0:m, 0:m]).then_inc(S["xe_ps"], 1)

                def expert(n, u, cnt, nxt):
                    pe.wait_ge(we_in[u], 32 * (cnt + 1))
                    pe.wait_ge(S["xe_ready"], n + 1)
                    for ft in range(FT):
                        mm(hbank[ft][:, 0:CAP], W1[u][:, P * ft:P * ft + P], xeT[:], start=True, stop=True).then_inc(S["h_ps"], 1)
                    if nxt:
                        tokens(n + 1, 1 - u, cnt + u)
                    ybank = (pj0, pj1)[u]
                    for j, m in enumerate((P, P, CAP - 2 * P)):
                        for ft in range(FT):
                            if j == 0:
                                pe.wait_ge(S["h_ready"], FT * n + ft + 1)
                            last = mm(ybank[0:m, P * j:P * j + P], hT[:, ft, P * j:P * j + m], W2[u][:, ft, :],
                                      start=ft == 0, stop=ft == FT - 1)
                    last.then_inc(S["y_ps"], 1)

                n0, c0 = E * phase, E // 2 * phase
                tokens(n0, 0, c0)
                with pe.Fori(0, E // 2 - 1) as ee:
                    expert(n0 + 2 * ee, 0, c0 + ee, True)
                    expert(n0 + 2 * ee + 1, 1, c0 + ee, True)
                expert(n0 + E - 2, 0, c0 + E // 2 - 1, True)
                expert(n0 + E - 1, 1, c0 + E // 2 - 1, False)

            pe.wait_ge(S["consts"], 1)
            pe.wait_ge(S["rows_in"], 80)
            nc.tensor.transpose(pj0[:, 0:ROWS], rows[:], identf[0:ROWS, 0:ROWS]).then_inc(S["rt_ps"], 1)
            pe.wait_ge(S["rt_ready"], 1)
            route(0)
            experts(0)
            with pe.Fori(0, NG) as g:
                transpose_group(NG + g)

            def wpart(w, lowpart, r):
                return (WL if lowpart else WH)[:, bass.ds(1024 * w + P * r, P)]

            TERMS = ((0, 0), (1, 0), (0, 1))

            def qk(f, b, r, outs):
                pe.wait_ge(S["x_lo"], b + 1)
                pe.wait_ge(S["tv"], f)
                for w, ps, done in ((0, pj0, "q_ps"), (1, pj1, "k_ps")):
                    if w:
                        pe.wait_ge(S["tk"], f)
                        pe.wait_ge(S["yt"], outs + 1)
                    for t, (wl, xl) in enumerate(TERMS):
                        last = mm(ps[:], wpart(w, wl, r), (XL if xl else XH)[:, bass.ds(GN * b, GN)],
                                  start=t == 0, stop=t == 2)
                    last.then_inc(S[done], 1)

            def v(f, b, r):
                pe.wait_ge(S["tq"], f + 1)
                for t in range(GT):
                    o = pj0[:, P * t:P * t + P]
                    for k, (wl, xl) in enumerate(TERMS):
                        mm(o, (XL if xl else XH)[:, bass.ds(GN * b + P * t, P)], wpart(2, wl, r), start=k == 0, stop=False)
                    last = mm(o, onesb[:], bvs[:, bass.ds(P * r, P)], start=False, stop=True)
                last.then_inc(S["v_ps"], 1)

            def scores(i):
                pe.wait_ge(S["q_lo"], i + 1)
                pe.wait_ge(S["k_pad"], i + 1)
                for h in range(2):
                    for c, (a, n, kts) in enumerate(CHUNKS):
                        if h:
                            pe.wait_ge(S["exp_done"], 6 * i + c + 1)
                        for kt in kts:
                            o = KOFF[kt] - a
                            w = GN - P * kt
                            for t, (kl, ql) in enumerate(TERMS):
                                mm(sc[c][:, o:o + w], KP[h][:, kl, P * kt:P * kt + P], Qn[:, ql, P * kt:GN],
                                   start=t == 0, stop=False)
                            last = mm(sc[c][:, o:o + P], identb[:], maskn[:], start=False, stop=True)
                        last.then_inc(S["s_ps"], 1)

            def context(i, b):
                pe.wait_ge(S["v_lo"], i + 1)
                pe.wait_ge(S["x_added"], b + 1)
                for h in range(2):
                    pe.wait_ge(S["p_hi"], 6 * i + 3 * h + 3)
                    pe.wait_ge(S["p_lo_p"], len(POOL_CHUNKS) * (2 * i + h + 1))
                    pe.wait_ge(S["p_lo_v"], len(V_CHUNKS) * (2 * i + h + 1))
                    for qt in range(GT):
                        o = (HD + 1) * qt
                        for kt in range(qt + 1):
                            a = KOFF[kt] + P * (qt - kt)
                            mm(cx[h][:, o:o + HD + 1], Ph[h][:, a:a + P], Vh[:, kt, h, :], start=kt == 0, stop=False)
                            mm(cx[h][:, o:o + HD], Ph[h][:, a:a + P], Vl[:, kt, h, :], start=False, stop=False)
                            last = mm(cx[h][:, o:o + HD + 1], Pl[h][:, a:a + P], Vh[:, kt, h, :], start=False, stop=kt == qt)
                    last.then_inc(S["ctx_ps"], 1)

            def context_t(i):
                pe.wait_ge(S["ctxn"], 2 * i + 2)
                pe.wait_ge(S["ct_lo"], i + 1)
                for t in range(GT):
                    last = nc.tensor.transpose(tT[:, P * t:P * t + P], cn[:, t, :], identf[:])
                last.then_inc(S["ct_ps"], 1)

            def step(i, b, nb, nr):
                scores(i)
                if nb is not None:
                    qk(i + 1, nb, nr, b)
                context(i, b)
                if nb is not None:
                    v(i + 1, nb, nr)
                context_t(i)

            def batch(b, last):
                with pe.Fori(0, NPAIR - 1) as j:
                    step(NPAIR * b + j, b, b, j + 1)
                step(NPAIR * b + NPAIR - 1, b, None if last else b + 1, 0)
                pe.wait_ge(S["tk"], NPAIR * b + NPAIR + (0 if last else 1))
                for r in range(NPAIR):
                    if r == NPAIR - 1:
                        pe.wait_ge(S["ct_lo"], NPAIR * b + NPAIR + 1)
                    for t, (wl, cl) in enumerate(TERMS):
                        last_mm = mm(pj1[:], (WL if wl else WH)[:, 3072 + P * r:3072 + P * r + P], CT[:, r, cl, :],
                                     start=r == 0 and t == 0, stop=r == NPAIR - 1 and t == 2)
                last_mm.then_inc(S["wo_ps"], 1)
                pe.wait_ge(S["yt"], b + 2)
                for t in range(GT):
                    last_mm = nc.tensor.transpose(cA[:, P * t:P * t + P], yT[:, P * t:P * t + P], identf[:])
                last_mm.then_inc(S["yt_ps"], 1)

            pe.wait_ge(S["w_split"], E)
            pe.wait_ge(S["bv_ready"], 3)
            pe.wait_ge(S["ks_init"], 1)
            qk(0, 0, 0, 0)
            v(0, 0, 0)
            with pe.Fori(0, NG - 1) as b:
                batch(b, False)
            batch(NG - 1, True)
            route(1)
            experts(1)

        @block.vector
        def _(dve):
            for s in CREDITED["vector"]:
                dve.sem_inc(s, 1)

            def layernorm(n, g, wait_kept):
                s = Steps(dve, S["ln_step"], LN_STEPS * n, LN_STEPS)
                xt = [X[:, bass.ds(GT * g + t, 1), :].rearrange("p a d -> p (a d)") for t in range(GT)]
                for t in range(GT):
                    last = dve.bn_stats(st[:, t, :], xt[t])
                s.done(last)
                dve.memset(spare[:], 0.0)
                for t in range(GT):
                    last = dve.bn_aggr(mv[:, t, :], st[:, t, :])
                s.done(last)
                dve.tensor_scalar(ve[:], mv[:, :, 1], EPS, None, ALU.add).then_inc(S["var_ready"], 1)
                dve.wait_ge(S["rs_pow"], n + 1)
                s.done(dve.tensor_tensor(ra[:], r0[:], r0[:], ALU.mult))
                s.done(dve.scalar_tensor_tensor(rb[:], ra[:], -0.5, ve[:], ALU.mult, ALU.mult))
                s.done(dve.scalar_tensor_tensor(rstd[:], rb[:], 1.5, r0[:], ALU.add, ALU.mult))
                if wait_kept is not None:
                    dve.wait_ge(S["xn_kept"], wait_kept + 1)
                dve.wait_ge(S["xt_ps"], n + 1)
                for t in range(GT):
                    last = dve.tensor_scalar(xn[:, t, :], xt[t], mv[:, t, 0:1], rstd[:, t:t + 1], ALU.subtract, ALU.mult)
                last.then_inc(S["xn_ready"], 1)
                s.end()

            def route(phase):
                dve.memset(carry[:], 0.0).then_inc(S["carry0"], 1)
                dve.wait_ge(S["carry0"], phase + 1)
                with dve.Fori(0, NG) as g:
                    n = NG * phase + g
                    layernorm(8 * phase + g, g, n)
                    s = Steps(dve, S["route_step"], ROUTE_STEPS * n, ROUTE_STEPS)
                    lg = pj0[:, 0:GT * E].rearrange("p (t e) -> p t e", e=E)
                    wide = lambda a: a.unsqueeze(2).broadcast_to([P, GT, E])
                    dve.wait_ge(S["logit_ps"], n + 1)
                    s.done(dve.tensor_reduce(mx[:], lg, X_AXIS, ALU.max))
                    dve.tensor_tensor(dl[:], lg, wide(mx[:]), ALU.subtract).then_inc(S["dl_ready"], 1)
                    dve.wait_ge(S["dl_ready"], n + 1)
                    s.done(dve.tensor_scalar(m0[:], dl[:], 0.0, None, ALU.is_equal))
                    s.done(dve.tensor_tensor(ms[:], m0[:], pick[:].unsqueeze(1).broadcast_to([P, GT, E]), ALU.mult))
                    s.done(dve.tensor_reduce(m2[:], ms[:], X_AXIS, ALU.max))
                    dve.tensor_tensor(mask[:], ms[:], wide(m2[:]), ALU.is_equal).then_inc(S["mask_ready"], 1)
                    dve.wait_ge(S["el_ready"], n + 1)
                    s.done(dve.tensor_reduce(se[:], el[:], X_AXIS, ALU.add))
                    s.done(dve.reciprocal(pr[:], se[:]))
                    dve.wait_ge(S["rank_ps"], n + 1)
                    s.done(dve.tensor_tensor(pos[:], pj1[:, 0:GT * E].rearrange("p (t e) -> p t e", e=E),
                                             carry[:].unsqueeze(1).broadcast_to([P, GT, E]), ALU.add))
                    dve.tensor_tensor(AB[:, 0], pos[:], mask[:], ALU.mult)
                    dve.tensor_tensor(AB[:, 1], ebase[:].unsqueeze(1).broadcast_to([P, GT, E]), mask[:], ALU.mult)
                    s.done(dve.tensor_tensor(carry[:], carry[:], pj1[:, 64:64 + E], ALU.add))
                    s.done(dve.tensor_reduce(rs[:], AB[:], X_AXIS, ALU.add))
                    dve.tensor_scalar(keep[:], rs[:, 0], float(CAP), None, ALU.is_le)
                    s.done(dve.tensor_tensor(slot[:], rs[:, 0], rs[:, 1], ALU.add))
                    tk_ = tok[:, bass.ds(GT * g, GT)]
                    s.done(dve.tensor_tensor(sd[:], slot[:], tk_, ALU.subtract))
                    s.done(dve.tensor_tensor(sk[:], sd[:], keep[:], ALU.mult))
                    dve.tensor_tensor(idx_s[:, bass.ds(GT * g, GT)], sk[:], tk_, ALU.add).then_inc(S["idx_ready"], 1)
                    s.done(dve.tensor_tensor(idx_g[:, bass.ds(GT * g, GT)], slot[:], keep[:], ALU.mult))
                    s.done(dve.scalar_tensor_tensor(wts[:, bass.ds(GT * g, GT)], pr[:], 0.5, keep[:], ALU.mult, ALU.mult))
                    s.end()

            def experts(phase):
                def tokens(n):
                    dve.wait_ge(S["xe_ps"], n + 1)
                    dve.tensor_copy(xeT[:], tT[:, 0:CAP]).then_inc(S["xe_ready"], 1)

                def outputs(n, e, u, cnt):
                    yb = (pj0, pj1)[u]
                    dve.wait_ge(S["y_ps"], n + 1)
                    dve.wait_ge(y_st[u], 32 * cnt + 1)
                    m = CAP - 2 * P
                    bias = b2bc[:, bass.ds(P * e, P)]
                    dve.tensor_tensor(Y[u][:, 0:2, :], yb[:, 0:2 * P].rearrange("p (j d) -> p j d", j=2),
                                      bias.unsqueeze(1).broadcast_to([P, 2, P]), ALU.add)
                    dve.tensor_tensor(Y[u][0:m, 2, :], yb[0:m, 2 * P:3 * P], b2bc[0:m, bass.ds(P * e, P)],
                                      ALU.add).then_inc(S["y_ready"], 1)

                def split_weights(e):
                    part = bass.ds(512 * e, 512)
                    dve.tensor_scalar(WH[:, part], Wf[:, part], am[:, 4:5], None, ALU.mult).then_inc(S["w_ready"], 1)
                    dve.wait_ge(S["w_ready"], e + 1)
                    dve.scalar_tensor_tensor(WL[:, part], Wf[:, part], am[:, 4:5], WH[:, part], ALU.mult,
                                             ALU.subtract).then_inc(S["w_split"], 1)

                n0, c0 = E * phase, E // 2 * phase
                tokens(n0)

                def pair(ee, last):
                    for u in range(2):
                        e = 2 * ee + u
                        if not (last and u):
                            tokens(n0 + e + 1)
                        if phase == 0:
                            split_weights(e)
                        outputs(n0 + e, e, u, c0 + ee)

                with dve.Fori(0, E // 2 - 1) as ee:
                    pair(ee, False)
                pair(E // 2 - 1, True)

            def combine(phase, g, static_g):
                for t in range(GT):
                    xt = X[:, bass.ds(GT * g + t, 1), :]
                    last = dve.scalar_tensor_tensor(xt, G[:, bass.ds(GT * g + t, 1), :], wts[:, bass.ds(GT * g + t, 1)],
                                                    xt, ALU.mult, ALU.add)
                last.then_inc(S["combined"], 1)

            dve.memset(KP[0][HD:P, :, :], 0.0)
            dve.memset(KP[1][0:HD, :, :], 0.0)
            dve.wait_ge(S["consts"], 1)
            dve.wait_ge(S["x_in"], 16)
            route(0)
            dve.wait_ge(S["w_in"], 64)
            s = Steps(dve, S["wscale"], 0, 8)
            s.done(dve.tensor_reduce(am[:, 0:1], Wf[:], X_AXIS, ALU.max))
            s.done(dve.tensor_reduce(am[:, 6:7], Wf[:], X_AXIS, ALU.min))
            s.done(dve.tensor_scalar(am[:, 7:8], am[:, 6:7], -1.0, None, ALU.mult))
            dve.tensor_tensor(am[:, 0:1], am[:, 0:1], am[:, 7:8], ALU.max).then_inc(S["amax"], 1)
            dve.wait_ge(S["amax_all"], 1)
            s.done(dve.tensor_scalar(am[:, 2:3], am[:, 1:2], 1e-30, None, ALU.max))
            s.done(dve.tensor_scalar(am[:, 3:4].bitcast(U32), am[:, 2:3].bitcast(U32), 0x7F800000, None, ALU.bitwise_and))
            s.done(dve.reciprocal(am[:, 6:7], am[:, 3:4]))
            s.done(dve.tensor_scalar(am[:, 4:5], am[:, 6:7], 2.0 ** 14, None, ALU.mult))
            s.done(dve.tensor_scalar(am[:, 5:6], am[:, 3:4], 2.0 ** -14, None, ALU.mult))
            s.end()
            dve.wait_ge(S["b2_in"], 16)
            experts(0)
            dve.wait_ge(S["bv_in"], 48)
            dve.wait_ge(S["ks_init"], 1)
            s = Steps(dve, S["bv_ready"], 0, 8)
            s.done(dve.tensor_scalar(bvr[:], bvf[:], am[:, 4:5], None, ALU.mult))
            s.done(dve.tensor_copy(bvt[:], bvr[:]))
            s.done(dve.tensor_tensor(bvf[:], bvr[:], bvt[:], ALU.subtract))
            s.done(dve.tensor_copy(bvu[:], bvf[:]))
            s.done(dve.tensor_tensor(bvr[:], bvf[:], bvu[:], ALU.subtract))
            s.done(dve.tensor_copy(bvs[0:32, :], bvt[0:32, :]))
            s.done(dve.tensor_copy(bvs[32:64, :], bvu[32:64, :]))
            s.done(dve.tensor_copy(bvs[64:96, :], bvr[64:96, :]))
            s.end()
            for g in range(NG):
                dve.wait_ge(gsem[g], 64)
                combine(0, g, True)
                dve.wait_ge(S["combined"], g + 1)
                layernorm(NG + g, g, NG if g == 0 else None)
                dve.wait_ge(S["x_hi"], g + 1)
                dve.tensor_tensor(XL[:, GN * g:GN * g + GN], tT[:], XH[:, GN * g:GN * g + GN], ALU.subtract).then_inc(S["x_lo"], 1)

            def qk_high(f):
                dve.wait_ge(S["tq"], f + 1)
                dve.tensor_copy(Qn[:, 0, :], Tq[:]).then_inc(S["q_hi"], 1)
                dve.wait_ge(S["tk"], f + 1)
                dve.tensor_copy(Kn[:, 0, :], Tk[:]).then_inc(S["k_hi"], 1)

            def k_pad(f):
                dve.wait_ge(S["k_hi"], f + 1)
                dve.wait_ge(S["k_lo"], f + 1)
                dve.tensor_copy(KP[0][0:HD, :, :], Kn[0:HD, :, :])
                dve.tensor_copy(KP[1][HD:P, :, :], Kn[HD:P, :, :]).then_inc(S["k_pad"], 1)

            def v_high(f):
                dve.wait_ge(S["tv"], f + 1)
                dve.tensor_copy(Vh[:, :, :, 0:HD], Tv[:].rearrange("p (t h d) -> p t h d", t=GT, h=2)).then_inc(S["v_hi"], 1)

            def normalise(i, h):
                c = cx[h][:, 0:GT * (HD + 1)].rearrange("p (t d) -> p t d", d=HD + 1)
                dve.wait_ge(S["ctx_ps"], 2 * i + h + 1)
                dve.reciprocal(rden[h][:], c[:, :, HD]).then_inc(S["rden_ready"], 1)
                dve.wait_ge(S["rden_ready"], 2 * i + h + 1)
                dve.tensor_tensor(cn[:, :, HD * h:HD * h + HD], c[:, :, 0:HD],
                                  rden[h][:].unsqueeze(2).broadcast_to([P, GT, HD]), ALU.mult).then_inc(S["ctxn"], 1)

            def step(i, r, nxt):
                for h in range(2):
                    for c, (a, n, _) in enumerate(CHUNKS):
                        dve.wait_ge(S["exp_done"], 6 * i + 3 * h + c + 1)
                        dve.tensor_copy(Ph[h][:, a:a + n], Pf[h][:, a:a + n]).then_inc(S["p_hi"], 1)
                        if c in V_CHUNKS:
                            dve.wait_ge(S["p_hi"], 6 * i + 3 * h + c + 1)
                            dve.tensor_tensor(Pl[h][:, a:a + n], Pf[h][:, a:a + n], Ph[h][:, a:a + n],
                                              ALU.subtract).then_inc(S["p_lo_v"], 1)
                if nxt:
                    qk_high(i + 1)
                normalise(i, 0)
                if nxt:
                    k_pad(i + 1)
                normalise(i, 1)
                if nxt:
                    v_high(i + 1)
                dve.wait_ge(S["ct_hi"], i + 1)
                dve.tensor_tensor(CT[:, bass.ds(r, 1), 1, :], tT[:].unsqueeze(1), CT[:, bass.ds(r, 1), 0, :], ALU.subtract).then_inc(S["ct_lo"], 1)

            def batch(b, last):
                with dve.Fori(0, NPAIR - 1) as j:
                    step(NPAIR * b + j, j, True)
                step(NPAIR * b + NPAIR - 1, NPAIR - 1, not last)
                dve.wait_ge(S["yt_ps"], b + 1)
                xg = X[:, bass.ds(GT * b, GT), :]
                dve.tensor_tensor(xg, xg, cA[:].rearrange("p (t d) -> p t d", d=P), ALU.add).then_inc(S["x_added"], 1)

            qk_high(0)
            k_pad(0)
            v_high(0)
            with dve.Fori(0, NG - 1) as b:
                batch(b, False)
            batch(NG - 1, True)
            dve.wait_ge(S["x_added"], NG + 1)
            route(1)
            experts(1)
            for g in range(NG):
                dve.wait_ge(gsem[g], 128)
                combine(1, g, True)


_INS = ["L0_attn_states", "L0_attn_Wq", "L0_attn_bq", "L0_attn_Wk", "L0_attn_bk", "L0_attn_Wv", "L0_attn_bv",
        "L0_attn_Wo", "L0_attn_bo", "L0_ffn_gate_w", "L0_ffn_w1", "L0_ffn_b1", "L0_ffn_w2", "L0_ffn_b2"]


def kernel(**inputs):
    import concourse.bacc as bacc
    from concourse.bass_utils import run_bass_kernel_spmd

    nc = bacc.Bacc("TRN2", target_bir_lowering=False, num_devices=1)
    arrays, args = {}, []
    for name in _INS:
        a = np.ascontiguousarray(inputs[name])
        arrays[f"in_{name}"] = a
        args.append(nc.dram_tensor(f"in_{name}", a.shape, mybir.dt.from_np(a.dtype), kind="ExternalInput").ap())
    args.append(nc.dram_tensor("out", (4, 512, 128), F32, kind="ExternalOutput").ap())
    macaron(nc, *args)
    r = run_bass_kernel_spmd(nc, [arrays], core_ids=[0])
    return r.results[0]["out"]
```

```python
from contextlib import ExitStack

import numpy as np

import concourse.bass as bass
from concourse import mybir

F32 = mybir.dt.float32
F16 = mybir.dt.float16
BF16 = mybir.dt.bfloat16
U32 = mybir.dt.uint32
ALU = mybir.AluOpType
ACT = mybir.ActivationFunctionType
X_AXIS = mybir.AxisListType.X
ABSMAX = bass.bass_isa.ReduceOp.max

P = 128
NTOK = 2048
NT = 16
GT = 4
NG = NT // GT
GN = GT * P
ROW = P + 1
E = 8
CAP = 320
SLOTS = E * CAP
DFF = 512
FT = DFF // P
NPAIR = 8
HD = 64
EPS = 1e-5
NEG = -30000.0
LN_PSHIFT = float(np.log(16.0))
LN_STEPS = 5
ROUTE_STEPS = 13
KOFF = [0, 512, 1024, 896]
CHUNKS = [(0, 512, [0]), (512, 512, [1, 3]), (1024, 256, [2])]
POOL_CHUNKS = [0]
V_CHUNKS = [1, 2]
B1_COL, BQ_COL, BK_COL, BO_COL, GW_COL, ROWS = 0, 32, 40, 48, 49, 57


class Steps:

    def __init__(self, eng, sem, base, total):
        self.eng, self.sem, self.base, self.total, self.k = eng, sem, base, total, 0

    def done(self, ins):
        self.k += 1
        ins.then_inc(self.sem, 1)
        self.eng.wait_ge(self.sem, self.base + self.k)

    def end(self):
        assert self.k == self.total, (self.k, self.total)


def macaron(nc, x_d, wq, bq, wk, bk, wv, bv, wo, bo, gate_w, w1, b1, w2, b2, out):
    ctx = ExitStack()
    with ctx:
        def sb(name, shape, dt):
            return ctx.enter_context(nc.sbuf_tensor(name, shape, dt))

        def bank(name):
            return ctx.enter_context(nc.psum_tensor(name, [P, 512], F32))

        def sem(name):
            return ctx.enter_context(nc.semaphore(name))

        disp = [nc.dram_tensor(f"disp{k}", [SLOTS + NTOK, ROW], F32, kind="Internal").ap() for k in range(2)]
        ytok = [nc.dram_tensor(f"ytok{k}", [NTOK + SLOTS, P], F32, kind="Internal").ap() for k in range(2)]
        x_v = x_d.rearrange("b s d -> (b s) d").rearrange("(t p) d -> p t d", p=P)
        out_v = out.rearrange("b s d -> (b s) d").rearrange("(t p) d -> p t d", p=P)
        y_v = [y[0:NTOK, :].rearrange("(t p) d -> p t d", p=P) for y in ytok]

        X = sb("X", [P, NT, P], F32)
        XN = sb("XN", [P, NT, ROW], F32)
        xa = sb("xa", [P, GT, P], F32)
        G = sb("G", [P, NT, P], F32)
        xT = sb("xT", [P, NT * P], F32)
        XH = sb("XH", [P, NT * P], F16)
        XL = sb("XL", [P, NT * P], F16)
        Wf = sb("Wf", [P, 4096], F32)
        WH = sb("WH", [P, 4096], F16)
        WL = sb("WL", [P, 4096], F16)
        bvf = sb("bvf", [P, 1024], F32)
        bvs = sb("bvs", [P, 1024], BF16)
        b2bc = sb("b2bc", [P, E * P], F32)
        rows = sb("rows", [ROWS, P], F32)
        RT = sb("RT", [P, ROWS], F32)
        empty = sb("empty", [P, SLOTS // P, ROW], F32)
        identf = sb("identf", [P, P], F32)
        identb = sb("identb", [P, P], BF16)
        onesb = sb("onesb", [P, P], BF16)
        lower = sb("lower", [P, P], BF16)
        maskn = sb("maskn", [P, P], BF16)
        pick = sb("pick", [P, E], F32)
        ebase = sb("ebase", [P, E], F32)
        tok = sb("tok", [P, NT], F32)
        number = sb("number", [P, NT], U32)
        mhalf = sb("mhalf", [P, NT], F32)
        pshift = sb("pshift", [P, 1], F32)
        spare = sb("spare", [P, 1], F32)
        st = sb("st", [P, NT, 6], F32)
        mv = sb("mv", [P, NT, 2], F32)
        ve = sb("ve", [P, NT], F32)
        r0 = sb("r0", [P, NT], F32)
        ra = sb("ra", [P, NT], F32)
        rb = sb("rb", [P, NT], F32)
        rstd = sb("rstd", [P, NT], F32)
        mx = sb("mx", [P, NT], F32)
        dl = sb("dl", [P, NT, E], F32)
        el = sb("el", [P, NT, E], F32)
        m0 = sb("m0", [P, NT, E], F32)
        ms = sb("ms", [P, NT, E], F32)
        m2 = sb("m2", [P, NT], F32)
        mask = sb("mask", [P, NT, E], BF16)
        se = sb("se", [P, NT], F32)
        pr = sb("pr", [P, NT], F32)
        pos = sb("pos", [P, NT, E], F32)
        ranks = sb("ranks", [P, NT, E], F32)
        bases = sb("bases", [P, NT, E], F32)
        rank = sb("rank", [P, NT], F32)
        base = sb("base", [P, NT], F32)
        keep = sb("keep", [P, NT], F32)
        slot = sb("slot", [P, NT], F32)
        sd = sb("sd", [P, NT], F32)
        sk = sb("sk", [P, NT], F32)
        carry = sb("carry", [P, E], F32)
        wts = sb("wts", [P, NT], F32)
        idx = sb("idx", [P, NT], U32)
        XE = [sb(f"XE{u}", [P, 3, ROW], F32) for u in range(2)]
        who = [sb(f"who{u}", [P, 3], U32) for u in range(2)]
        W1 = [sb(f"W1_{u}", [P, DFF], F32) for u in range(2)]
        W2 = [sb(f"W2_{u}", [P, FT, P], F32) for u in range(2)]
        xeT = sb("xeT", [P, CAP], F32)
        hT = sb("hT", [P, FT, CAP], F32)
        Y = [sb(f"Y{u}", [P, 3, P], F32) for u in range(2)]
        am = sb("am", [P, 8], F32)
        Tq = sb("Tq", [P, GN], F32)
        Tk = sb("Tk", [P, GN], F32)
        Tv = sb("Tv", [P, GN], F32)
        Qn = [sb(f"Qn{u}", [P, 2, GN], F16) for u in range(2)]
        Kn = sb("Kn", [P, 2, GN], F16)
        KP = [[sb(f"KP{u}{h}", [P, 2, GN], F16) for h in range(2)] for u in range(2)]
        Vh = [sb(f"Vh{u}", [P, GT, 2, HD + 1], F16) for u in range(2)]
        Vl = [sb(f"Vl{u}", [P, GT, 2, HD], F16) for u in range(2)]
        Pf = [sb(f"Pf{h}", [P, 1280], F32) for h in range(2)]
        Ph = [[sb(f"Ph{u}{h}", [P, 1280], F16) for h in range(2)] for u in range(2)]
        Pl = [[sb(f"Pl{u}{h}", [P, 1280], F16) for h in range(2)] for u in range(2)]
        bvr, bvt, bvu = Pf[0][:, 0:1024], Ph[0][0][:, 0:1024].bitcast(BF16), Ph[0][1][:, 0:1024].bitcast(BF16)
        rden = [sb(f"rden{h}", [P, GT], F32) for h in range(2)]
        cn = sb("cn", [P, GT, P], F32)
        CT = sb("CT", [P, NPAIR, 2, GN], F16)
        yT = sb("yT", [P, GN], F32)

        sc = [bank(f"sc{i}") for i in range(3)]
        pj0, pj1, cA, cB, tT = bank("pj0"), bank("pj1"), bank("cA"), bank("cB"), bank("tT")
        cx = [cA, cB]
        hbank = [sc[0], sc[1], sc[2], cA]

        names = """x_in w_in rows_in b2_in bv_in slots_empty consts bvs_zero bv_zero pool_const rt_ps rt_ready
            carry0 ln_step var_ready rs_pow xn_ready xa_ready xa_ps xt_ps xt_ready
            logit_ps dl_ready el_ready mask_ready rank_ps route_step idx_ready scattered
            we_in0 we_in1 xe_in0 xe_in1 xe_ps xe_ready h_ps h_ready y_ps y_ready y_sc0 y_sc1
            combined passed amax amax_all wscale bv_ready w_split w_ready
            q_ps k_ps v_ps tq tk tv q_hi k_hi v_hi q_lo k_lo v_lo k_pad
            s_ps exp_done p_hi p_lo_v p_lo_p ctx_ps rden_ready ctxn ct_ps ct_hi ct_lo wo_ps yt yt_ps x_added
            x_hi x_lo out_done""".split()
        S = {n: sem(n) for n in names}
        we_in, xe_in, y_sc = [S["we_in0"], S["we_in1"]], [S["xe_in0"], S["xe_in1"]], [S["y_sc0"], S["y_sc1"]]
        gsem = [sem(f"gathered{g}") for g in range(NG)]
        block = ctx.enter_context(nc.Block())

        @block.sync
        def _(sp):
            def load_weights(e, u):
                sp.dma_start(W1[u][:], w1[bass.ds(e, 1), :, :].rearrange("a d f -> (a d) f")).then_inc(we_in[u], 16)
                sp.dma_start(W2[u][:], w2[bass.ds(e, 1), :, :].rearrange("a (t p) d -> p (a t) d", p=P)).then_inc(we_in[u], 16)

            def load_tokens(e, u, phase):
                d = disp[phase]
                sp.dma_start(XE[u][:, 0:2, :], d[bass.ds(e * CAP, 2 * P), :].rearrange("(p j) d -> p j d", j=2)).then_inc(xe_in[u], 16)
                sp.dma_start(XE[u][0:CAP - 2 * P, 2, :], d[bass.ds(e * CAP + 2 * P, CAP - 2 * P), :]).then_inc(xe_in[u], 16)

            def fill(phase):
                sp.dma_start(disp[phase][0:SLOTS, :].rearrange("(p j) d -> p j d", p=P), empty[:]).then_inc(S["slots_empty"], 16)
                sp.dma_start(ytok[phase][0:NTOK, :].rearrange("(p j) d -> p j d", p=P), empty[:, 0:NT, 0:P]).then_inc(S["slots_empty"], 16)

            sp.dma_start(X[:, :, :], x_v).then_inc(S["x_in"], 16)
            for phase in range(2):
                if phase:
                    sp.wait_ge(S["y_ps"], E)
                else:
                    sp.wait_ge(S["consts"], 2)
                    fill(0)
                load_weights(0, 0)
                load_weights(1, 1)
                if phase:
                    fill(1)
                sp.wait_ge(S["scattered"], 16 * NT * (phase + 1))
                load_tokens(0, 0, phase)
                load_tokens(1, 1, phase)
                with sp.Fori(0, E // 2 - 1) as ee:
                    for u in range(2):
                        n = E * phase + 2 * ee + u
                        sp.wait_ge(S["y_ps"], n + 1)
                        load_weights(2 * ee + u + 2, u)
                        load_tokens(2 * ee + u + 2, u, phase)
                for u in range(2):
                    sp.wait_ge(y_sc[u], 48 * (E // 2) * (phase + 1))
                for g in range(NG):
                    sp.dma_start(G[:, GT * g:GT * g + GT, :], y_v[phase][:, GT * g:GT * g + GT, :]).then_inc(gsem[g], 16)
            with sp.Fori(0, NG) as g:
                sp.wait_ge(S["combined"], NG + 1 + g)
                sp.dma_start(out_v[:, bass.ds(GT * g, GT), :], X[:, bass.ds(GT * g, GT), :]).then_inc(S["out_done"], 16)
            sp.wait_ge(S["out_done"], 16 * NG)

        @block.gpsimd
        def _(pool):
            pool.memset(mhalf[:], -0.5)
            pool.memset(identf[:], 0.0).then_inc(S["pool_const"], 1)
            pool.memset(identb[:], 0.0).then_inc(S["pool_const"], 1)
            pool.memset(onesb[:], 1.0).then_inc(S["pool_const"], 1)
            pool.memset(maskn[:], 0.0).then_inc(S["pool_const"], 1)
            pool.memset(lower[:], 1.0).then_inc(S["pool_const"], 1)
            pool.wait_ge(S["pool_const"], 5)
            for m in (identf, identb):
                pool.affine_select(out=m[:], in_=m[:], compare_op=ALU.not_equal, fill=1.0, base=0,
                                   pattern=[[-1, P]], channel_multiplier=1)
            pool.affine_select(out=maskn[:], in_=maskn[:], compare_op=ALU.is_ge, fill=NEG, base=0,
                               pattern=[[1, P]], channel_multiplier=-1)
            pool.affine_select(out=lower[:], in_=lower[:], compare_op=ALU.is_ge, fill=0.0, base=0,
                               pattern=[[1, P]], channel_multiplier=-1)
            pool.iota(pick[:], [[-1, E]], base=E, channel_multiplier=0, allow_small_or_imprecise_dtypes=True)
            pool.iota(ebase[:], [[CAP, E]], base=-1, channel_multiplier=0, allow_small_or_imprecise_dtypes=True)
            pool.iota(tok[:], [[P, NT]], base=SLOTS, channel_multiplier=1, allow_small_or_imprecise_dtypes=True)
            pool.iota(number[:], [[P, NT]], base=0, channel_multiplier=1)
            pool.memset(pshift[:], LN_PSHIFT).then_inc(S["consts"], 1)
            pool.memset(empty[:], 0.0).then_inc(S["pool_const"], 1)
            pool.wait_ge(S["pool_const"], 6)
            pool.iota(empty[:, :, P:ROW].bitcast(U32), [[1, SLOTS // P], [1, 1]], base=NTOK,
                      channel_multiplier=SLOTS // P).then_inc(S["consts"], 1)

            def inv_std(n, tiles, done):
                pool.wait_ge(S["var_ready"], n + 1)
                pool.tensor_tensor(r0[:, 0:tiles], ve[:, 0:tiles], mhalf[:, 0:tiles], ALU.pow).then_inc(done, 1)

            def dispatch(n, phase, tiles):
                pool.wait_ge(S["idx_ready"], n + 1)
                pool.sem_inc(S["passed"], 1)
                for t in range(tiles):
                    pool.indirect_dma_start(disp[phase], bass.IndirectOffsetOnAxis(ap=idx[:, t:t + 1], axis=0),
                                            XN[:, t, :], None).then_inc(S["scattered"], 16)

            def experts(phase):
                with pool.Fori(0, E // 2) as ee:
                    for u in range(2):
                        pool.wait_ge(S["y_ready"], E * phase + 2 * ee + u + 1)
                        pool.sem_inc(S["passed"], 1)
                        for j in range(3):
                            m = min(P, CAP - P * j)
                            pool.indirect_dma_start(ytok[phase], bass.IndirectOffsetOnAxis(ap=who[u][0:m, j:j + 1], axis=0),
                                                    Y[u][0:m, j, :], None).then_inc(y_sc[u], 16)

            inv_std(0, NT, S["rs_pow"])
            pool.memset(bvf[:], 0.0).then_inc(S["bv_zero"], 1)
            pool.memset(bvs[:], 0.0).then_inc(S["bvs_zero"], 1)
            for u in range(2):
                pool.memset(Vh[u][:, :, :, HD:HD + 1], 1.0)
            pool.wait_ge(S["slots_empty"], 32)
            dispatch(0, 0, NT)
            pool.wait_ge(S["amax"], 1)
            pool.partition_all_reduce(am[:, 1:2], am[:, 0:1], P, ABSMAX).then_inc(S["amax_all"], 1)
            experts(0)

            def low(dst, src, hi, done):
                pool.tensor_tensor(dst, src, hi, ALU.subtract).then_inc(done, 1)

            def qk_low(i, u):
                pool.wait_ge(S["q_hi"], i + 1)
                low(Qn[u][:, 1, :], Tq[:], Qn[u][:, 0, :], S["q_lo"])
                pool.wait_ge(S["k_hi"], i + 1)
                low(Kn[:, 1, :], Tk[:], Kn[:, 0, :], S["k_lo"])

            def v_low(i, u):
                pool.wait_ge(S["v_hi"], i + 1)
                low(Vl[u][:], Tv[:].rearrange("p (t h d) -> p t h d", t=GT, h=2), Vh[u][:, :, :, 0:HD], S["v_lo"])

            def p_low(s, u):
                for h in range(2):
                    for c in POOL_CHUNKS:
                        a, n, _ = CHUNKS[c]
                        pool.wait_ge(S["p_hi"], 6 * s + 3 * h + c + 1)
                        low(Pl[u][h][:, a:a + n], Pf[h][:, a:a + n], Ph[u][h][:, a:a + n], S["p_lo_p"])

            def step(b, r, project=True, score=True):
                i, u = NPAIR * b + r, r % 2
                if project:
                    qk_low(i, u)
                if score:
                    p_low(i - 1, 1 - u)
                if project:
                    v_low(i, u)

            inv_std(1, GT, S["rs_pow"])
            for r in range(NPAIR):
                step(0, r, score=r > 0)
                if r < NG - 1:
                    inv_std(2 + r, GT, S["rs_pow"])
            pool.wait_ge(S["slots_empty"], 64)
            with pool.Fori(1, NG) as b:
                for r in range(NPAIR):
                    step(b, r)
                    if r == 3:
                        inv_std(NG + b, GT, S["rs_pow"])
                dispatch(b, 1, GT)
            step(NG, 0, project=False)
            inv_std(2 * NG, GT, S["rs_pow"])
            dispatch(NG, 1, GT)
            experts(1)

        @block.scalar
        def _(act):
            act.sem_inc(S["yt"], 1)
            act.dma_start(rows[B1_COL:B1_COL + 32, :], b1.rearrange("e (t p) -> (e t) p", p=P)).then_inc(S["rows_in"], 16)
            act.dma_start(rows[BQ_COL:BQ_COL + 8, :], bq.rearrange("(r p) -> r p", p=P)).then_inc(S["rows_in"], 16)
            act.dma_start(rows[BK_COL:BK_COL + 8, :], bk.rearrange("(r p) -> r p", p=P)).then_inc(S["rows_in"], 16)
            act.dma_start(rows[BO_COL:BO_COL + 1, :], bo.rearrange("(r p) -> r p", p=P)).then_inc(S["rows_in"], 16)
            act.dma_start(rows[GW_COL:GW_COL + 8, :], gate_w).then_inc(S["rows_in"], 16)
            act.dma_start(b2bc[:], b2.rearrange("e d -> (e d)").partition_broadcast(P)).then_inc(S["b2_in"], 16)
            act.wait_ge(S["rt_ps"], 1)
            act.activation(RT[:], pj0[:, 0:ROWS], ACT.Copy).then_inc(S["rt_ready"], 1)
            for k, w in enumerate((wq, wk, wv)):
                act.dma_start(Wf[:, 1024 * k:1024 * (k + 1)], w).then_inc(S["w_in"], 16)
            act.dma_start(Wf[:, 3072:4096].rearrange("p (r d) -> p r d", d=P), wo.rearrange("(r p) d -> p r d", p=P)).then_inc(S["w_in"], 16)

            def experts(phase):
                with act.Fori(0, E) as e:
                    for ft in range(FT):
                        act.wait_ge(S["h_ps"], FT * (E * phase + e) + ft + 1)
                        act.activation(hT[:, ft, :], hbank[ft][:, 0:CAP], ACT.Relu,
                                       bias=RT[:, bass.ds(B1_COL + FT * e + ft, 1)]).then_inc(S["h_ready"], 1)

            def copy_xt(n, g, ps):
                act.wait_ge(S["xt_ps"], n + 1)
                act.activation(xT[:, GN * g:GN * g + GN], ps[:], ACT.Copy).then_inc(S["xt_ready"], 1)

            def exp_logits(n, tiles):
                act.wait_ge(S["dl_ready"], n + 1)
                act.activation(el[:, 0:tiles], dl[:, 0:tiles], ACT.Exp).then_inc(S["el_ready"], 1)

            def split_x(g):
                act.wait_ge(S["xa_ps"], g + 1)
                act.activation(XH[:, GN * g:GN * g + GN], cB[:], ACT.Copy).then_inc(S["x_hi"], 1)

            for g in range(NG):
                copy_xt(g, g, sc[g % 2])
            exp_logits(0, NT)
            for k in range(3):
                if k == 0:
                    act.wait_ge(S["bv_zero"], 1)
                act.dma_start(bvf[32 * k:32 * k + 1, :], bv.rearrange("(a n) -> a n", a=1)).then_inc(S["bv_in"], 16)
            experts(0)
            split_x(0)

            unscale = am[:, 5:6]

            def tanh_qk(i, r):
                first = isinstance(i, int) and i == 0
                act.wait_ge(S["q_ps"], i + 1)
                if not first:
                    act.wait_ge(S["q_lo"], i)
                act.activation(Tq[:], pj0[:], ACT.Tanh, bias=RT[:, BQ_COL + r:BQ_COL + r + 1], scale=unscale).then_inc(S["tq"], 1)
                act.wait_ge(S["k_ps"], i + 1)
                if not first:
                    act.wait_ge(S["k_lo"], i)
                act.activation(Tk[:], pj1[:], ACT.Tanh, bias=RT[:, BK_COL + r:BK_COL + r + 1], scale=unscale).then_inc(S["tk"], 1)

            def tanh_v(i):
                act.wait_ge(S["v_ps"], i + 1)
                if not (isinstance(i, int) and i == 0):
                    act.wait_ge(S["v_lo"], i)
                act.activation(Tv[:], pj0[:], ACT.Tanh, scale=unscale).then_inc(S["tv"], 1)

            def exps(s):
                for h in range(2):
                    for c, (a, n, _) in enumerate(CHUNKS):
                        act.wait_ge(S["s_ps"], 6 * s + 3 * h + c + 1)
                        if not (isinstance(s, int) and s == 0):
                            if c in POOL_CHUNKS:
                                act.wait_ge(S["p_lo_p"], len(POOL_CHUNKS) * (2 * (s - 1) + h) + POOL_CHUNKS.index(c) + 1)
                            else:
                                act.wait_ge(S["p_lo_v"], len(V_CHUNKS) * (2 * (s - 1) + h) + V_CHUNKS.index(c) + 1)
                        act.activation(Pf[h][:, a:a + n], sc[c][:, 0:n], ACT.Exp, scale=0.125,
                                       bias=pshift[:]).then_inc(S["exp_done"], 1)

            def ct_high(t, r):
                act.wait_ge(S["ct_ps"], t + 1)
                act.activation(CT[:, r, 0, :], tT[:], ACT.Copy).then_inc(S["ct_hi"], 1)

            def out_tanh(b):
                act.wait_ge(S["wo_ps"], b + 1)
                act.activation(yT[:], cB[:], ACT.Tanh, bias=RT[:, BO_COL:BO_COL + 1], scale=unscale).then_inc(S["yt"], 1)

            def step(b, r, project=True, score=True, turn=True):
                i = NPAIR * b + r
                if turn:
                    ct_high(i - 3, (r - 3) % NPAIR)
                if project:
                    tanh_qk(i, r)
                if score:
                    exps(i - 1)
                if project:
                    tanh_v(i)

            for r in range(NPAIR):
                step(0, r, score=r > 0, turn=r > 2)
                if r < NG - 1:
                    split_x(r + 1)
            with act.Fori(1, NG) as b:
                for r in range(NPAIR):
                    step(b, r)
                    if r == 2:
                        out_tanh(b - 1)
                    if r == 5:
                        copy_xt(NG - 1 + b, 0, cA)
                    if r == 6:
                        exp_logits(b, GT)
            step(NG, 0, project=False)
            ct_high(NPAIR * NG - 2, NPAIR - 2)
            ct_high(NPAIR * NG - 1, NPAIR - 1)
            out_tanh(NG - 1)
            copy_xt(2 * NG - 1, 0, cA)
            exp_logits(NG, GT)
            experts(1)

        @block.tensor
        def _(pe):
            mm = nc.tensor.matmul

            def transpose_group(src, ps, done):
                for t in range(GT):
                    last = nc.tensor.transpose(ps[:, P * t:P * t + P], src[:, t, 0:P], identf[:])
                last.then_inc(done, 1)

            def logits(g, ps, done):
                for t in range(GT):
                    o = E * (GT * g + t)
                    last = mm(ps[:, o:o + E], xT[:, P * (GT * g + t):P * (GT * g + t) + P], RT[:, GW_COL:GW_COL + E],
                              start=True, stop=True)
                if done:
                    last.then_inc(S["logit_ps"], 1)

            def rank_tokens(n, tiles, ps):
                pe.wait_ge(S["mask_ready"], n + 1)
                mm(ps[:, 0:tiles * E], lower[:], mask[:, 0:tiles, :].rearrange("p t e -> p (t e)"), start=True, stop=False)
                for t in range(tiles - 1):
                    mm(ps[:, E * (t + 1):tiles * E].rearrange("p (t e) -> p t e", e=E), onesb[:],
                       mask[:, t:t + 1, :].broadcast_to([P, tiles - 1 - t, E]), start=False, stop=t == tiles - 2)
                for t in range(tiles):
                    last = mm(ps[:, 256:256 + E], onesb[:], mask[:, t, :], start=t == 0, stop=t == tiles - 1)
                last.then_inc(S["rank_ps"], 1)

            def experts(phase):
                def tokens(n, u, cnt):
                    pe.wait_ge(xe_in[u], 32 * (cnt + 1))
                    nc.tensor.transpose(tT[:, 0:P], XE[u][:, 0, 0:P], identf[:])
                    nc.tensor.transpose(tT[:, P:2 * P], XE[u][:, 1, 0:P], identf[:])
                    m = CAP - 2 * P
                    nc.tensor.transpose(tT[:, 2 * P:CAP], XE[u][0:m, 2, 0:P], identf[0:m, 0:m]).then_inc(S["xe_ps"], 1)

                def expert(n, u, cnt, nxt):
                    pe.wait_ge(we_in[u], 32 * (cnt + 1))
                    pe.wait_ge(S["xe_ready"], n + 1)
                    for ft in range(FT):
                        mm(hbank[ft][:, 0:CAP], W1[u][:, P * ft:P * ft + P], xeT[:], start=True, stop=True).then_inc(S["h_ps"], 1)
                    if nxt:
                        tokens(n + 1, 1 - u, cnt + u)
                    ybank = (pj0, pj1)[u]
                    for j, m in enumerate((P, P, CAP - 2 * P)):
                        for ft in range(FT):
                            if j == 0:
                                pe.wait_ge(S["h_ready"], FT * n + ft + 1)
                            last = mm(ybank[0:m, P * j:P * j + P], hT[:, ft, P * j:P * j + m], W2[u][:, ft, :],
                                      start=ft == 0, stop=ft == FT - 1)
                    last.then_inc(S["y_ps"], 1)

                n0, c0 = E * phase, E // 2 * phase
                tokens(n0, 0, c0)
                with pe.Fori(0, E // 2 - 1) as ee:
                    expert(n0 + 2 * ee, 0, c0 + ee, True)
                    expert(n0 + 2 * ee + 1, 1, c0 + ee, True)
                expert(n0 + E - 2, 0, c0 + E // 2 - 1, True)
                expert(n0 + E - 1, 1, c0 + E // 2 - 1, False)

            pe.wait_ge(S["consts"], 1)
            pe.wait_ge(S["rows_in"], 80)
            nc.tensor.transpose(pj0[:, 0:ROWS], rows[:], identf[0:ROWS, 0:ROWS]).then_inc(S["rt_ps"], 1)
            pe.wait_ge(S["rt_ready"], 1)
            for g in range(NG):
                pe.wait_ge(S["xn_ready"], g + 1)
                if g >= 2:
                    pe.wait_ge(S["xt_ready"], g - 1)
                transpose_group(XN[:, GT * g:GT * g + GT], sc[g % 2], S["xt_ps"])
            for g in range(NG):
                pe.wait_ge(S["xt_ready"], g + 1)
                logits(g, pj0, g == NG - 1)
            rank_tokens(0, NT, pj1)
            experts(0)

            def norm_x(g):
                pe.wait_ge(S["xa_ready"], g + 1)
                if g:
                    pe.wait_ge(S["x_lo"], g)
                transpose_group(xa, cB, S["xa_ps"])

            norm_x(0)

            def wpart(w, lowpart, r):
                return (WL if lowpart else WH)[:, 1024 * w + P * r:1024 * w + P * r + P]

            TERMS = ((0, 0), (1, 0), (0, 1))

            def qk(i, b, r):
                first = isinstance(i, int) and i == 0
                if r == 0:
                    pe.wait_ge(S["x_lo"], b + 1)
                if not first:
                    pe.wait_ge(S["tv"], i)
                for w, ps, done in ((0, pj0, "q_ps"), (1, pj1, "k_ps")):
                    if w and not first:
                        pe.wait_ge(S["tk"], i)
                    for t, (wl, xl) in enumerate(TERMS):
                        last = mm(ps[:], wpart(w, wl, r), (XL if xl else XH)[:, bass.ds(GN * b, GN)],
                                  start=t == 0, stop=t == 2)
                    last.then_inc(S[done], 1)

            def v(i, b, r):
                pe.wait_ge(S["tq"], i + 1)
                for t in range(GT):
                    o = pj0[:, P * t:P * t + P]
                    for k, (wl, xl) in enumerate(TERMS):
                        mm(o, (XL if xl else XH)[:, bass.ds(GN * b + P * t, P)], wpart(2, wl, r), start=k == 0, stop=False)
                    last = mm(o, onesb[:], bvs[:, P * r:P * r + P], start=False, stop=True)
                last.then_inc(S["v_ps"], 1)

            def scores(s, u):
                pe.wait_ge(S["q_lo"], s + 1)
                pe.wait_ge(S["k_pad"], s + 1)
                for h in range(2):
                    for c, (a, n, kts) in enumerate(CHUNKS):
                        if h:
                            pe.wait_ge(S["exp_done"], 6 * s + c + 1)
                        elif not (isinstance(s, int) and s == 0):
                            pe.wait_ge(S["exp_done"], 6 * (s - 1) + 3 + c + 1)
                        for kt in kts:
                            o = KOFF[kt] - a
                            w = GN - P * kt
                            for t, (kl, ql) in enumerate(TERMS):
                                mm(sc[c][:, o:o + w], KP[u][h][:, kl, P * kt:P * kt + P], Qn[u][:, ql, P * kt:GN],
                                   start=t == 0, stop=False)
                            last = mm(sc[c][:, o:o + P], identb[:], maskn[:], start=False, stop=True)
                        last.then_inc(S["s_ps"], 1)

            def context(c, u):
                pe.wait_ge(S["v_lo"], c + 1)
                for h in range(2):
                    pe.wait_ge(S["p_hi"], 6 * c + 3 * h + 3)
                    pe.wait_ge(S["p_lo_p"], len(POOL_CHUNKS) * (2 * c + h + 1))
                    pe.wait_ge(S["p_lo_v"], len(V_CHUNKS) * (2 * c + h + 1))
                    for qt in range(GT):
                        o = (HD + 1) * qt
                        for kt in range(qt + 1):
                            a = KOFF[kt] + P * (qt - kt)
                            mm(cx[h][:, o:o + HD + 1], Ph[u][h][:, a:a + P], Vh[u][:, kt, h, :], start=kt == 0, stop=False)
                            mm(cx[h][:, o:o + HD], Ph[u][h][:, a:a + P], Vl[u][:, kt, h, :], start=False, stop=False)
                            last = mm(cx[h][:, o:o + HD + 1], Pl[u][h][:, a:a + P], Vh[u][:, kt, h, :], start=False, stop=kt == qt)
                    last.then_inc(S["ctx_ps"], 1)

            def context_t(t):
                pe.wait_ge(S["ctxn"], 2 * t + 2)
                pe.wait_ge(S["ct_lo"], t + 1)
                transpose_group(cn, tT, S["ct_ps"])

            def project_out(b, pairs):
                pe.wait_ge(S["ctxn"], 2 * pairs)
                for r in range(NPAIR):
                    if r == NPAIR - 1:
                        pe.wait_ge(S["ct_lo"], NPAIR * b + NPAIR + 1)
                    for t, (wl, cl) in enumerate(TERMS):
                        last = mm(cB[:], (WL if wl else WH)[:, 3072 + P * r:3072 + P * r + P], CT[:, r, cl, :],
                                  start=r == 0 and t == 0, stop=r == NPAIR - 1 and t == 2)
                last.then_inc(S["wo_ps"], 1)

            def turn_out(b, pairs):
                pe.wait_ge(S["yt"], b + 2)
                pe.wait_ge(S["ctxn"], 2 * pairs)
                for t in range(GT):
                    last = nc.tensor.transpose(cA[:, P * t:P * t + P], yT[:, P * t:P * t + P], identf[:])
                last.then_inc(S["yt_ps"], 1)

            def step(b, r, project=True, score=True, mix=True, turn=True):
                i, u = NPAIR * b + r, r % 2
                if turn:
                    context_t(i - 3)
                if project:
                    qk(i, b, r)
                if score:
                    scores(i - 1, 1 - u)
                if mix:
                    if isinstance(b, int) and b == 0:
                        if r <= NG:
                            pe.wait_ge(S["x_lo"], min(r + 1, NG))
                    else:
                        if r == 3:
                            pe.wait_ge(S["yt"], b + 1)
                        if r == 4:
                            pe.wait_ge(S["x_added"], b)
                        if r == 6:
                            pe.wait_ge(S["xt_ready"], NG + b)
                        if r == 7:
                            pe.wait_ge(S["dl_ready"], b + 1)
                        if r == 0:
                            pe.wait_ge(S["idx_ready"], b)
                    context(i - 2, u)
                if project:
                    v(i, b, r)

            pe.wait_ge(S["w_split"], E)
            pe.wait_ge(S["bv_ready"], 8)
            for r in range(NPAIR):
                step(0, r, score=r > 0, mix=r > 1, turn=r > 2)
                if r < NG - 1:
                    if r > 1:
                        pe.wait_ge(S["ctxn"], 2 * (r - 1))
                    norm_x(r + 1)
            with pe.Fori(1, NG) as b:
                for r in range(NPAIR):
                    step(b, r)
                    i = NPAIR * b + r
                    if r == 2:
                        project_out(b - 1, i - 1)
                    if r == 3:
                        turn_out(b - 1, i - 1)
                    if r == 5:
                        pe.wait_ge(S["xn_ready"], NG + b)
                        pe.wait_ge(S["ctxn"], 2 * (i - 1))
                        transpose_group(XN, cA, S["xt_ps"])
                    if r == 6:
                        pe.wait_ge(S["xt_ready"], NG + b)
                        pe.wait_ge(S["ctxn"], 2 * (i - 1))
                        logits(0, cA, True)
                    if r == 7:
                        pe.wait_ge(S["ctxn"], 2 * (i - 1))
                        rank_tokens(b, GT, cB)
            step(NG, 0, project=False)
            pairs = NPAIR * NG
            context_t(pairs - 2)
            context(pairs - 1, 1)
            context_t(pairs - 1)
            project_out(NG - 1, pairs)
            turn_out(NG - 1, pairs)
            pe.wait_ge(S["xn_ready"], 2 * NG)
            pe.wait_ge(S["x_added"], NG)
            transpose_group(XN, cA, S["xt_ps"])
            pe.wait_ge(S["xt_ready"], 2 * NG)
            logits(0, cA, True)
            rank_tokens(NG, GT, cB)
            experts(1)

        @block.vector
        def _(dve):
            dve.sem_inc(S["ct_lo"], 1)
            cnt = {"ln": 0}

            def ln_stats(n, first_tile, tiles):
                s = Steps(dve, S["ln_step"], LN_STEPS * n, LN_STEPS)
                dve.memset(spare[:], 0.0)
                for t in range(tiles):
                    last = dve.bn_stats(st[:, t, :], X[:, bass.ds(first_tile + t, 1), :].rearrange("p a d -> p (a d)"))
                s.done(last)
                dve.memset(spare[:], 0.0)
                for t in range(tiles):
                    last = dve.bn_aggr(mv[:, t, :], st[:, t, :])
                s.done(last)
                dve.tensor_scalar(ve[:, 0:tiles], mv[:, 0:tiles, 1], EPS, None, ALU.add).then_inc(S["var_ready"], 1)
                return s

            def ln_scale(n, s, tiles):
                dve.wait_ge(S["rs_pow"], n + 1)
                a = slice(0, tiles)
                s.done(dve.tensor_tensor(ra[:, a], r0[:, a], r0[:, a], ALU.mult))
                s.done(dve.scalar_tensor_tensor(rb[:, a], ra[:, a], -0.5, ve[:, a], ALU.mult, ALU.mult))
                s.done(dve.scalar_tensor_tensor(rstd[:, a], rb[:, a], 1.5, r0[:, a], ALU.add, ALU.mult))
                s.end()

            def ln_apply(dst, first_tile, k0, tiles, done):
                for t in range(tiles):
                    xt = X[:, bass.ds(first_tile + t, 1), :].rearrange("p a d -> p (a d)")
                    last = dve.tensor_scalar(dst[:, t, 0:P], xt, mv[:, k0 + t, 0:1], rstd[:, k0 + t:k0 + t + 1],
                                             ALU.subtract, ALU.mult)
                last.then_inc(done, 1)

            def choose(s, n, tiles, ps):
                a = slice(0, tiles)
                lg = ps[:, 0:tiles * E].rearrange("p (t e) -> p t e", e=E)
                wide = lambda v: v[:, a].unsqueeze(2).broadcast_to([P, tiles, E])
                dve.wait_ge(S["logit_ps"], n + 1)
                s.done(dve.tensor_reduce(mx[:, a], lg, X_AXIS, ALU.max))
                dve.tensor_tensor(dl[:, a], lg, wide(mx), ALU.subtract).then_inc(S["dl_ready"], 1)
                dve.wait_ge(S["dl_ready"], n + 1)
                s.done(dve.tensor_scalar(m0[:, a], dl[:, a], 0.0, None, ALU.is_equal))
                s.done(dve.tensor_tensor(ms[:, a], m0[:, a], pick[:].unsqueeze(1).broadcast_to([P, tiles, E]), ALU.mult))
                s.done(dve.tensor_reduce(m2[:, a], ms[:, a], X_AXIS, ALU.max))
                dve.tensor_tensor(mask[:, a], ms[:, a], wide(m2), ALU.is_equal).then_inc(S["mask_ready"], 1)

            def place(s, n, first_tile, tiles, ps):
                a = slice(0, tiles)
                every = lambda v: v[:].unsqueeze(1).broadcast_to([P, tiles, E])
                tiles_at = bass.ds(first_tile, tiles)
                dve.wait_ge(S["el_ready"], n + 1)
                s.done(dve.tensor_reduce(se[:, a], el[:, a], X_AXIS, ALU.add))
                s.done(dve.reciprocal(pr[:, a], se[:, a]))
                dve.wait_ge(S["mask_ready"], n + 1)
                dve.wait_ge(S["rank_ps"], n + 1)
                dve.tensor_tensor(bases[:, a], every(ebase), mask[:, a], ALU.mult)
                s.done(dve.tensor_tensor(pos[:, a], ps[:, 0:tiles * E].rearrange("p (t e) -> p t e", e=E), every(carry), ALU.add))
                dve.tensor_reduce(base[:, a], bases[:, a], X_AXIS, ALU.add)
                dve.tensor_tensor(carry[:], carry[:], ps[:, 256:256 + E], ALU.add)
                s.done(dve.tensor_tensor(ranks[:, a], pos[:, a], mask[:, a], ALU.mult))
                s.done(dve.tensor_reduce(rank[:, a], ranks[:, a], X_AXIS, ALU.add))
                dve.tensor_scalar(keep[:, a], rank[:, a], float(CAP), None, ALU.is_le)
                s.done(dve.tensor_tensor(slot[:, a], rank[:, a], base[:, a], ALU.add))
                s.done(dve.tensor_tensor(sd[:, a], slot[:, a], tok[:, tiles_at], ALU.subtract))
                s.done(dve.tensor_tensor(sk[:, a], sd[:, a], keep[:, a], ALU.mult))
                s.done(dve.scalar_tensor_tensor(wts[:, tiles_at], pr[:, a], 0.5, keep[:, a], ALU.mult, ALU.mult))
                dve.tensor_tensor(idx[:, a], sk[:, a], tok[:, tiles_at], ALU.add).then_inc(S["idx_ready"], 1)
                s.end()

            def experts(phase):
                m = CAP - 2 * P

                def tokens(n, u, cnt):
                    dve.wait_ge(xe_in[u], 32 * (cnt + 1))
                    if not (isinstance(cnt, int) and cnt == 0):
                        dve.wait_ge(y_sc[u], 48 * cnt)
                    dve.tensor_copy(who[u][:, 0:2], XE[u][:, 0:2, P:ROW].rearrange("p j a -> p (j a)").bitcast(U32))
                    dve.tensor_copy(who[u][0:m, 2:3], XE[u][0:m, 2, P:ROW].bitcast(U32))
                    dve.wait_ge(S["xe_ps"], n + 1)
                    dve.tensor_copy(xeT[:], tT[:, 0:CAP]).then_inc(S["xe_ready"], 1)

                def outputs(n, e, u):
                    yb = (pj0, pj1)[u]
                    dve.wait_ge(S["y_ps"], n + 1)
                    bias = b2bc[:, bass.ds(P * e, P)]
                    dve.tensor_tensor(Y[u][:, 0:2, :], yb[:, 0:2 * P].rearrange("p (j d) -> p j d", j=2),
                                      bias.unsqueeze(1).broadcast_to([P, 2, P]), ALU.add)
                    dve.tensor_tensor(Y[u][0:m, 2, :], yb[0:m, 2 * P:3 * P], b2bc[0:m, bass.ds(P * e, P)],
                                      ALU.add).then_inc(S["y_ready"], 1)

                def split_weights(e):
                    part = bass.ds(512 * e, 512)
                    dve.tensor_scalar(WH[:, part], Wf[:, part], am[:, 4:5], None, ALU.mult).then_inc(S["w_ready"], 1)
                    dve.wait_ge(S["w_ready"], e + 1)
                    dve.scalar_tensor_tensor(WL[:, part], Wf[:, part], am[:, 4:5], WH[:, part], ALU.mult,
                                             ALU.subtract).then_inc(S["w_split"], 1)

                n0, c0 = E * phase, E // 2 * phase
                tokens(n0, 0, c0)

                def pair(ee, last):
                    for u in range(2):
                        e = 2 * ee + u
                        if not (last and u):
                            tokens(n0 + e + 1, 1 - u, c0 + ee + u)
                        if phase == 0:
                            split_weights(e)
                        outputs(n0 + e, e, u)

                pair(0, False)
                with dve.Fori(1, E // 2 - 1) as ee:
                    pair(ee, False)
                pair(E // 2 - 1, True)

            def combine(phase, g):
                dve.wait_ge(gsem[g], 16 * (phase + 1))
                for t in range(GT * g, GT * g + GT):
                    last = dve.scalar_tensor_tensor(X[:, t, :], G[:, t, :], wts[:, t:t + 1], X[:, t, :], ALU.mult, ALU.add)
                last.then_inc(S["combined"], 1)

            for u in range(2):
                dve.memset(KP[u][0][HD:P, :, :], 0.0)
                dve.memset(KP[u][1][0:HD, :, :], 0.0)
            dve.memset(carry[:], 0.0).then_inc(S["carry0"], 1)
            dve.wait_ge(S["x_in"], 16)
            s = ln_stats(0, 0, NT)
            ln_scale(0, s, NT)
            for g in range(NG):
                ln_apply(XN[:, GT * g:GT * g + GT], GT * g, GT * g, GT, S["xn_ready"])
            dve.wait_ge(S["consts"], 2)
            dve.wait_ge(S["carry0"], 1)
            dve.tensor_copy(XN[:, :, P:ROW].rearrange("p t a -> p (t a)").bitcast(U32), number[:])
            s = Steps(dve, S["route_step"], 0, ROUTE_STEPS)
            choose(s, 0, NT, pj0)
            place(s, 0, 0, NT, pj1)
            dve.memset(carry[:], 0.0).then_inc(S["carry0"], 1)
            dve.wait_ge(S["w_in"], 64)
            s = Steps(dve, S["wscale"], 0, 8)
            s.done(dve.tensor_reduce(am[:, 0:1], Wf[:], X_AXIS, ALU.max))
            s.done(dve.tensor_reduce(am[:, 6:7], Wf[:], X_AXIS, ALU.min))
            s.done(dve.tensor_scalar(am[:, 7:8], am[:, 6:7], -1.0, None, ALU.mult))
            dve.tensor_tensor(am[:, 0:1], am[:, 0:1], am[:, 7:8], ALU.max).then_inc(S["amax"], 1)
            dve.wait_ge(S["amax_all"], 1)
            s.done(dve.tensor_scalar(am[:, 2:3], am[:, 1:2], 1e-30, None, ALU.max))
            s.done(dve.tensor_scalar(am[:, 3:4].bitcast(U32), am[:, 2:3].bitcast(U32), 0x7F800000, None, ALU.bitwise_and))
            s.done(dve.reciprocal(am[:, 6:7], am[:, 3:4]))
            s.done(dve.tensor_scalar(am[:, 4:5], am[:, 6:7], 2.0 ** 14, None, ALU.mult))
            s.done(dve.tensor_scalar(am[:, 5:6], am[:, 3:4], 2.0 ** -14, None, ALU.mult))
            s.end()
            dve.wait_ge(S["b2_in"], 16)
            experts(0)
            dve.wait_ge(S["bv_in"], 48)
            dve.wait_ge(S["bvs_zero"], 1)
            s = Steps(dve, S["bv_ready"], 0, 8)
            s.done(dve.tensor_scalar(bvr, bvf[:], am[:, 4:5], None, ALU.mult))
            s.done(dve.tensor_copy(bvt, bvr))
            s.done(dve.tensor_tensor(bvf[:], bvr, bvt, ALU.subtract))
            s.done(dve.tensor_copy(bvu, bvf[:]))
            s.done(dve.tensor_tensor(bvr, bvf[:], bvu, ALU.subtract))
            s.done(dve.tensor_copy(bvs[0:32, :], bvt[0:32, :]))
            s.done(dve.tensor_copy(bvs[32:64, :], bvu[32:64, :]))
            s.done(dve.tensor_copy(bvs[64:96, :], bvr[64:96, :]))
            s.end()

            def norm_x(g):
                combine(0, g)
                dve.wait_ge(S["combined"], g + 1)
                s = ln_stats(1 + g, GT * g, GT)
                ln_scale(1 + g, s, GT)
                if g:
                    dve.wait_ge(S["xa_ps"], g)
                ln_apply(xa, GT * g, 0, GT, S["xa_ready"])
                dve.wait_ge(S["x_hi"], g + 1)
                dve.tensor_tensor(XL[:, GN * g:GN * g + GN], cB[:], XH[:, GN * g:GN * g + GN], ALU.subtract).then_inc(S["x_lo"], 1)

            norm_x(0)

            def qk_high(i, u):
                dve.wait_ge(S["tq"], i + 1)
                dve.tensor_copy(Qn[u][:, 0, :], Tq[:]).then_inc(S["q_hi"], 1)
                dve.wait_ge(S["tk"], i + 1)
                dve.tensor_copy(Kn[:, 0, :], Tk[:]).then_inc(S["k_hi"], 1)

            def k_pad(i, u):
                dve.wait_ge(S["k_hi"], i + 1)
                dve.wait_ge(S["k_lo"], i + 1)
                dve.tensor_copy(KP[u][0][0:HD, :, :], Kn[0:HD, :, :])
                dve.tensor_copy(KP[u][1][HD:P, :, :], Kn[HD:P, :, :]).then_inc(S["k_pad"], 1)

            def v_high(i, u):
                dve.wait_ge(S["tv"], i + 1)
                dve.tensor_copy(Vh[u][:, :, :, 0:HD], Tv[:].rearrange("p (t h d) -> p t h d", t=GT, h=2)).then_inc(S["v_hi"], 1)

            def split_p(s, u, between):
                late = []
                for h in range(2):
                    for c, (a, n, _) in enumerate(CHUNKS):
                        k = 6 * s + 3 * h + c + 1
                        dve.wait_ge(S["exp_done"], k)
                        dve.tensor_copy(Ph[u][h][:, a:a + n], Pf[h][:, a:a + n]).then_inc(S["p_hi"], 1)
                        if late:
                            lk, lh, la, ln = late.pop()
                            dve.wait_ge(S["p_hi"], lk)
                            dve.tensor_tensor(Pl[u][lh][:, la:la + ln], Pf[lh][:, la:la + ln], Ph[u][lh][:, la:la + ln],
                                              ALU.subtract).then_inc(S["p_lo_v"], 1)
                        if c in V_CHUNKS:
                            late.append((k, h, a, n))
                        if (h, c) in between:
                            between[h, c]()
                lk, lh, la, ln = late.pop()
                dve.wait_ge(S["p_hi"], lk)
                dve.tensor_tensor(Pl[u][lh][:, la:la + ln], Pf[lh][:, la:la + ln], Ph[u][lh][:, la:la + ln],
                                  ALU.subtract).then_inc(S["p_lo_v"], 1)

            def normalise(c):
                heads = [cx[h][:, 0:GT * (HD + 1)].rearrange("p (t d) -> p t d", d=HD + 1) for h in range(2)]
                for h in range(2):
                    dve.wait_ge(S["ctx_ps"], 2 * c + h + 1)
                    dve.reciprocal(rden[h][:], heads[h][:, :, HD]).then_inc(S["rden_ready"], 1)
                    dve.wait_ge(S["rden_ready"], 2 * c + h + 1)
                    dve.tensor_tensor(cn[:, :, HD * h:HD * h + HD], heads[h][:, :, 0:HD],
                                      rden[h][:].unsqueeze(2).broadcast_to([P, GT, HD]), ALU.mult).then_inc(S["ctxn"], 1)

            def ct_low(t, r):
                dve.wait_ge(S["ct_hi"], t + 1)
                dve.tensor_tensor(CT[:, r, 1, :], tT[:], CT[:, r, 0, :], ALU.subtract).then_inc(S["ct_lo"], 1)

            def step(b, r, project=True, score=True, mix=True, turn=True):
                i, u = NPAIR * b + r, r % 2
                if turn:
                    ct_low(i - 3, (r - 3) % NPAIR)
                if project:
                    qk_high(i, u)
                pad = {(1, 0): lambda: k_pad(i, u)} if project else {}
                if score:
                    split_p(i - 1, 1 - u, pad)
                elif project:
                    k_pad(i, u)
                if mix:
                    normalise(i - 2)
                if project:
                    v_high(i, u)

            def add_out(b):
                dve.wait_ge(S["yt_ps"], b + 1)
                xg = X[:, bass.ds(GT * b, GT), :]
                dve.tensor_tensor(xg, xg, cA[:].rearrange("p (t d) -> p t d", d=P), ALU.add).then_inc(S["x_added"], 1)
                dve.wait_ge(S["x_added"], b + 1)

            def norm_batch(n, g, s):
                ln_scale(NG + n, s, GT)
                dve.wait_ge(S["scattered"], 16 * (NT + GT * g))
                dve.tensor_copy(XN[:, 0:GT, P:ROW].rearrange("p t a -> p (t a)").bitcast(U32), number[:, bass.ds(GT * g, GT)])
                ln_apply(XN, GT * g, 0, GT, S["xn_ready"])

            for r in range(NPAIR):
                step(0, r, score=r > 0, mix=r > 1, turn=r > 2)
                if r < NG - 1:
                    norm_x(r + 1)
            dve.wait_ge(S["carry0"], 2)
            with dve.Fori(1, NG) as b:
                for r in range(NPAIR):
                    step(b, r)
                    if r == 3:
                        add_out(b - 1)
                        ln = ln_stats(NG + b, GT * (b - 1), GT)
                    if r == 4:
                        norm_batch(b, b - 1, ln)
                    if r == 6:
                        s = Steps(dve, S["route_step"], ROUTE_STEPS * b, ROUTE_STEPS)
                        choose(s, b, GT, cA)
                    if r == 7:
                        place(s, b, GT * (b - 1), GT, cB)
            step(NG, 0, project=False)
            normalise(NPAIR * NG - 1)
            ct_low(NPAIR * NG - 2, NPAIR - 2)
            ct_low(NPAIR * NG - 1, NPAIR - 1)
            add_out(NG - 1)
            ln = ln_stats(2 * NG, GT * (NG - 1), GT)
            norm_batch(NG, NG - 1, ln)
            s = Steps(dve, S["route_step"], ROUTE_STEPS * NG, ROUTE_STEPS)
            choose(s, NG, GT, cA)
            place(s, NG, GT * (NG - 1), GT, cB)
            experts(1)
            for g in range(NG):
                combine(1, g)


_INS = ["L0_attn_states", "L0_attn_Wq", "L0_attn_bq", "L0_attn_Wk", "L0_attn_bk", "L0_attn_Wv", "L0_attn_bv",
        "L0_attn_Wo", "L0_attn_bo", "L0_ffn_gate_w", "L0_ffn_w1", "L0_ffn_b1", "L0_ffn_w2", "L0_ffn_b2"]


def kernel(**inputs):
    import concourse.bacc as bacc
    from concourse.bass_utils import run_bass_kernel_spmd

    nc = bacc.Bacc("TRN2", target_bir_lowering=False, num_devices=1)
    arrays, args = {}, []
    for name in _INS:
        a = np.ascontiguousarray(inputs[name])
        arrays[f"in_{name}"] = a
        args.append(nc.dram_tensor(f"in_{name}", a.shape, mybir.dt.from_np(a.dtype), kind="ExternalInput").ap())
    args.append(nc.dram_tensor("out", (4, 512, 128), F32, kind="ExternalOutput").ap())
    macaron(nc, *args)
    r = run_bass_kernel_spmd(nc, [arrays], core_ids=[0])
    return r.results[0]["out"]
```

```python
from contextlib import ExitStack

import numpy as np

import concourse.bass as bass
from concourse import mybir

F32 = mybir.dt.float32
F16 = mybir.dt.float16
BF16 = mybir.dt.bfloat16
U32 = mybir.dt.uint32
ALU = mybir.AluOpType
ACT = mybir.ActivationFunctionType
X_AXIS = mybir.AxisListType.X
ABSMAX = bass.bass_isa.ReduceOp.max

P = 128
NTOK = 2048
NT = 16
GT = 4
NG = NT // GT
GN = GT * P
FIRST = ((0, 4), (4, 4), (8, 8))
NS = len(FIRST)
ROW = P + 1
E = 8
CAP = 320
SLOTS = E * CAP
DFF = 512
FT = DFF // P
NPAIR = 8
HD = 64
EPS = 1e-5
NEG = -30000.0
LN_PSHIFT = float(np.log(16.0))
ROUTE_STEPS = 13
KOFF = [0, 512, 1024, 896]
CHUNKS = [(0, 512, [0]), (512, 512, [1, 3]), (1024, 256, [2])]
POOL_CHUNKS = [[0, 2], [0, 2]]
V_CHUNKS = [[1], [1]]
X_STATS, X_APPLY, X_TURN = {0: 2, 1: 3}, {0: 1, 1: 2, 2: 3}, {1: 1, 2: 2, 3: 3}
B1_COL, BQ_COL, BK_COL, BO_COL, GW_COL, ROWS = 0, 32, 40, 48, 49, 57


class Steps:

    def __init__(self, eng, sem, base, total):
        self.eng, self.sem, self.base, self.total, self.k = eng, sem, base, total, 0

    def done(self, ins):
        self.k += 1
        ins.then_inc(self.sem, 1)
        self.eng.wait_ge(self.sem, self.base + self.k)

    def end(self):
        assert self.k == self.total, (self.k, self.total)


def macaron(nc, x_d, wq, bq, wk, bk, wv, bv, wo, bo, gate_w, w1, b1, w2, b2, out):
    ctx = ExitStack()
    with ctx:
        def sb(name, shape, dt):
            return ctx.enter_context(nc.sbuf_tensor(name, shape, dt))

        def bank(name):
            return ctx.enter_context(nc.psum_tensor(name, [P, 512], F32))

        def sem(name):
            return ctx.enter_context(nc.semaphore(name))

        disp = [nc.dram_tensor(f"disp{k}", [SLOTS + NTOK, ROW], F32, kind="Internal").ap() for k in range(2)]
        ytok = [nc.dram_tensor(f"ytok{k}", [NTOK + SLOTS, P], F32, kind="Internal").ap() for k in range(2)]
        x_v = x_d.rearrange("b s d -> (b s) d").rearrange("(t p) d -> p t d", p=P)
        out_v = out.rearrange("b s d -> (b s) d").rearrange("(t p) d -> p t d", p=P)
        y_v = [y[0:NTOK, :].rearrange("(t p) d -> p t d", p=P) for y in ytok]

        X = sb("X", [P, NT, P], F32)
        XN = sb("XN", [P, NT, ROW], F32)
        xa = sb("xa", [P, GT, P], F32)
        G = sb("G", [P, NT, P], F32)
        xT = sb("xT", [P, NT * P], F32)
        XH = sb("XH", [P, NT * P], F16)
        XL = sb("XL", [P, NT * P], F16)
        Wf = sb("Wf", [P, 4096], F32)
        WH = sb("WH", [P, 4096], F16)
        WL = sb("WL", [P, 4096], F16)
        bvf = sb("bvf", [P, 1024], F32)
        bvs = sb("bvs", [P, 1024], BF16)
        b2bc = sb("b2bc", [P, E * P], F32)
        rows = sb("rows", [ROWS, P], F32)
        RT = sb("RT", [P, ROWS], F32)
        empty = sb("empty", [P, SLOTS // P, ROW], F32)
        identf = sb("identf", [P, P], F32)
        identb = sb("identb", [P, P], BF16)
        onesb = sb("onesb", [P, P], BF16)
        lower = sb("lower", [P, P], BF16)
        maskn = sb("maskn", [P, P], BF16)
        pick = sb("pick", [P, E], F32)
        ebase = sb("ebase", [P, E], F32)
        tok = sb("tok", [P, NT], F32)
        number = sb("number", [P, NT], U32)
        mhalf = sb("mhalf", [P, NT], F32)
        pshift = sb("pshift", [P, 1], F32)
        spare = sb("spare", [P, 1], F32)
        st = sb("st", [P, NT, 6], F32)
        mv = sb("mv", [P, NT, 2], F32)
        ve = sb("ve", [P, NT], F32)
        r0 = sb("r0", [P, NT], F32)
        ra = sb("ra", [P, NT], F32)
        rb = sb("rb", [P, NT], F32)
        rstd = sb("rstd", [P, NT], F32)
        mx = sb("mx", [P, NT], F32)
        dl = sb("dl", [P, NT, E], F32)
        el = sb("el", [P, NT, E], F32)
        m0 = sb("m0", [P, NT, E], F32)
        ms = sb("ms", [P, NT, E], F32)
        m2 = sb("m2", [P, NT], F32)
        mask = sb("mask", [P, NT, E], BF16)
        se = sb("se", [P, NT], F32)
        pr = sb("pr", [P, NT], F32)
        pos = sb("pos", [P, NT, E], F32)
        ranks = sb("ranks", [P, NT, E], F32)
        bases = sb("bases", [P, NT, E], F32)
        rank = sb("rank", [P, NT], F32)
        base = sb("base", [P, NT], F32)
        keep = sb("keep", [P, NT], F32)
        slot = sb("slot", [P, NT], F32)
        sd = sb("sd", [P, NT], F32)
        sk = sb("sk", [P, NT], F32)
        carry = sb("carry", [P, E], F32)
        wts = sb("wts", [P, NT], F32)
        idx = sb("idx", [P, NT], U32)
        XE = [sb(f"XE{u}", [P, 3, ROW], F32) for u in range(2)]
        nxt = [sb(f"nxt{u}", [P, 3], U32) for u in range(2)]
        who = [sb(f"who{u}", [P, 3], U32) for u in range(2)]
        W1 = [sb(f"W1_{u}", [P, DFF], F32) for u in range(2)]
        W2 = [sb(f"W2_{u}", [P, FT, P], F32) for u in range(2)]
        xeT = sb("xeT", [P, CAP], F32)
        hT = [sb(f"hT{u}", [P, FT, CAP], F32) for u in range(2)]
        Y = [sb(f"Y{u}", [P, 3, P], F32) for u in range(2)]
        am = sb("am", [P, 8], F32)
        Tq = sb("Tq", [P, GN], F32)
        Tk = sb("Tk", [P, GN], F32)
        Qn = [sb(f"Qn{u}", [P, 2, GN], F16) for u in range(2)]
        Kn = [sb(f"Kn{u}", [P, 2, GN], F16) for u in range(2)]
        QS = [[sb(f"QS{u}{h}", [P, GN], F16) for h in range(2)] for u in range(2)]
        KS = [[sb(f"KS{u}{h}", [P, 2, GN], F16) for h in range(2)] for u in range(2)]
        Vh = [sb(f"Vh{u}", [P, GT, 2, HD + 1], F16) for u in range(2)]
        Vl = [sb(f"Vl{u}", [P, GT, 2, HD], F16) for u in range(2)]
        Pf = [[sb(f"Pf{h}", [P, 1280], F32) for h in range(2)], [Wf[:, 1280 * h:1280 * (h + 1)] for h in range(2)]]
        Tv = [sb("Tv", [P, GN], F32), Wf[:, 2560:2560 + GN]]
        Ph = [[sb(f"Ph{u}{h}", [P, 1280], F16) for h in range(2)] for u in range(2)]
        Pl = [[sb(f"Pl{u}{h}", [P, 1280], F16) for h in range(2)] for u in range(2)]
        bvr, bvt, bvu = Pf[0][0][:, 0:1024], Ph[0][0][:, 0:1024].bitcast(BF16), Ph[0][1][:, 0:1024].bitcast(BF16)
        rden = [sb(f"rden{h}", [P, GT], F32) for h in range(2)]
        cn = sb("cn", [P, GT, P], F32)
        CT = sb("CT", [P, NPAIR, 2, GN], F16)
        yT = sb("yT", [P, GN], F32)

        sc = [bank(f"sc{i}") for i in range(3)]
        pj0, pj1, cA, cB, tT = bank("pj0"), bank("pj1"), bank("cA"), bank("cB"), bank("tT")
        cx = [cA, cB]
        hbank = [sc[0], sc[1], sc[2], cA]

        names = """w_in rows_in b2_in bv_in slots_empty consts bvs_zero bv_zero pool_const rt_ps rt_ready
            carry0 stat_step scale_step var_ready rs_pow xn_ready xa_ready xa_ps xt_ps xt_ready
            logit_ps dl_ready el_ready mask_ready rank_ps rank_read route_step idx_ready scattered
            w1_in0 w1_in1 w2_in0 w2_in1 xe_in0 xe_in1 xe_ps xe_ready h_ps h_ready y_ps y_ready y_sc0 y_sc1
            kept combined passed amax amax_all wscale bv_ready w_split w_ready
            q_ps k_ps v_ps tq tk tv q_hi k_hi v_hi q_lo k_lo v_lo own_half
            s_ps exp_done p_hi p_lo_v p_lo_p ctx_ps rden_ready ctxn ct_ps ct_hi ct_lo wo_ps yt yt_ps x_added
            x_hi x_lo out_done""".split()
        S = {n: sem(n) for n in names}
        w1_in, w2_in = [S["w1_in0"], S["w1_in1"]], [S["w2_in0"], S["w2_in1"]]
        xe_in, y_sc = [S["xe_in0"], S["xe_in1"]], [S["y_sc0"], S["y_sc1"]]
        half = lambda h: slice(HD * h, HD * h + HD)
        qs_in = [sem(f"qs_in{u}") for u in range(2)]
        ks_in = [sem(f"ks_in{u}") for u in range(2)]
        gsem = [sem(f"gathered{g}") for g in range(NG)]
        x_in = [sem(f"x_in{k}") for k in range(NS)]
        block = ctx.enter_context(nc.Block())

        def low_part(s, h, c):
            done, chunks = ("p_lo_p", POOL_CHUNKS) if c in POOL_CHUNKS[h] else ("p_lo_v", V_CHUNKS)
            return S[done], (len(chunks[0]) + len(chunks[1])) * s + len(chunks[0]) * h + chunks[h].index(c) + 1

        @block.sync
        def _(sp):
            def load_w1(e, u):
                sp.dma_start(W1[u][:], w1[bass.ds(e, 1), :, :].rearrange("a d f -> (a d) f")).then_inc(w1_in[u], 16)

            def load_w2(e, u):
                sp.dma_start(W2[u][:], w2[bass.ds(e, 1), :, :].rearrange("a (t p) d -> p (a t) d", p=P)).then_inc(w2_in[u], 16)

            def load_tokens(e, u, phase):
                d = disp[phase]
                sp.dma_start(XE[u][:, 0:2, :], d[bass.ds(e * CAP, 2 * P), :].rearrange("(p j) d -> p j d", j=2)).then_inc(xe_in[u], 16)
                sp.dma_start(XE[u][0:CAP - 2 * P, 2, :], d[bass.ds(e * CAP + 2 * P, CAP - 2 * P), :]).then_inc(xe_in[u], 16)

            def fill(phase):
                sp.dma_start(disp[phase][0:SLOTS, :].rearrange("(p j) d -> p j d", p=P), empty[:]).then_inc(S["slots_empty"], 16)
                sp.dma_start(ytok[phase][0:NTOK, :].rearrange("(p j) d -> p j d", p=P), empty[:, 0:NT, 0:P]).then_inc(S["slots_empty"], 16)

            def stack_heads(i, u):
                sp.wait_ge(S["q_hi"], i + 1)
                for h in range(2):
                    sp.dma_start(QS[u][h][half(h)], Qn[u][half(h), 0, :]).then_inc(qs_in[u], 16)
                sp.wait_ge(S["q_lo"], i + 1)
                for h in range(2):
                    sp.dma_start(QS[u][h][half(1 - h)], Qn[u][half(h), 1, :]).then_inc(qs_in[u], 16)
                sp.wait_ge(S["k_lo"], i + 1)
                for h in range(2):
                    sp.dma_start(KS[u][h][half(1 - h)], Kn[u][half(h)]).then_inc(ks_in[u], 16)

            for k, (t0, tiles) in enumerate(FIRST):
                sp.dma_start(X[:, t0:t0 + tiles, :], x_v[:, t0:t0 + tiles, :]).then_inc(x_in[k], 16)
            for phase in range(2):
                if phase:
                    sp.wait_ge(S["y_ps"], E)
                else:
                    sp.wait_ge(S["consts"], 2)
                    fill(0)
                for u in range(2):
                    load_w1(u, u)
                    load_w2(u, u)
                if phase:
                    fill(1)
                    with sp.Fori(0, NPAIR * NG // 2) as ii:
                        for u in range(2):
                            stack_heads(2 * ii + u, u)
                sp.wait_ge(S["scattered"], 16 * NT * (phase + 1))
                load_tokens(0, 0, phase)
                load_tokens(1, 1, phase)
                n0 = E * phase

                def first_layer(e, u):
                    sp.wait_ge(S["xe_ready"], n0 + e + 1)
                    load_tokens(e + 2, u, phase)
                    sp.wait_ge(S["h_ps"], FT * (n0 + e + 1))
                    load_w1(e + 2, u)

                def second_layer(e, u):
                    sp.wait_ge(S["y_ps"], n0 + e + 1)
                    load_w2(e + 2, u)

                first_layer(0, 0)
                with sp.Fori(0, E // 2 - 2) as ee:
                    first_layer(2 * ee + 1, 1)
                    second_layer(2 * ee, 0)
                    first_layer(2 * ee + 2, 0)
                    second_layer(2 * ee + 1, 1)
                first_layer(E - 3, 1)
                second_layer(E - 4, 0)
                second_layer(E - 3, 1)
                for u in range(2):
                    sp.wait_ge(y_sc[u], 48 * (E // 2) * (phase + 1))
                for g in range(NG):
                    sp.dma_start(G[:, GT * g:GT * g + GT, :], y_v[phase][:, GT * g:GT * g + GT, :]).then_inc(gsem[g], 16)
            with sp.Fori(0, NG) as g:
                sp.wait_ge(S["combined"], NG + 1 + g)
                sp.dma_start(out_v[:, bass.ds(GT * g, GT), :], X[:, bass.ds(GT * g, GT), :]).then_inc(S["out_done"], 16)
            sp.wait_ge(S["out_done"], 16 * NG)

        @block.gpsimd
        def _(pool):
            pool.memset(mhalf[:], -0.5)
            pool.memset(identf[:], 0.0).then_inc(S["pool_const"], 1)
            pool.memset(identb[:], 0.0).then_inc(S["pool_const"], 1)
            pool.memset(onesb[:], 1.0).then_inc(S["pool_const"], 1)
            pool.memset(maskn[:], 0.0).then_inc(S["pool_const"], 1)
            pool.memset(lower[:], 1.0).then_inc(S["pool_const"], 1)
            pool.wait_ge(S["pool_const"], 5)
            for m in (identf, identb):
                pool.affine_select(out=m[:], in_=m[:], compare_op=ALU.not_equal, fill=1.0, base=0,
                                   pattern=[[-1, P]], channel_multiplier=1)
            pool.affine_select(out=maskn[:], in_=maskn[:], compare_op=ALU.is_ge, fill=NEG, base=0,
                               pattern=[[1, P]], channel_multiplier=-1)
            pool.affine_select(out=lower[:], in_=lower[:], compare_op=ALU.is_ge, fill=0.0, base=0,
                               pattern=[[1, P]], channel_multiplier=-1)
            pool.iota(pick[:], [[-1, E]], base=E, channel_multiplier=0, allow_small_or_imprecise_dtypes=True)
            pool.iota(ebase[:], [[CAP, E]], base=-1, channel_multiplier=0, allow_small_or_imprecise_dtypes=True)
            pool.iota(tok[:], [[P, NT]], base=SLOTS, channel_multiplier=1, allow_small_or_imprecise_dtypes=True)
            pool.iota(number[:], [[P, NT]], base=0, channel_multiplier=1)
            pool.memset(pshift[:], LN_PSHIFT).then_inc(S["consts"], 1)
            pool.memset(empty[:], 0.0).then_inc(S["pool_const"], 1)
            pool.wait_ge(S["pool_const"], 6)
            pool.iota(empty[:, :, P:ROW].bitcast(U32), [[1, SLOTS // P], [1, 1]], base=NTOK,
                      channel_multiplier=SLOTS // P).then_inc(S["consts"], 1)

            def inv_std(n, k0, tiles):
                a = slice(k0, k0 + tiles)
                pool.wait_ge(S["var_ready"], n + 1)
                pool.tensor_tensor(r0[:, a], ve[:, a], mhalf[:, a], ALU.pow).then_inc(S["rs_pow"], 1)

            def dispatch(n, phase, k0, tiles):
                pool.wait_ge(S["idx_ready"], n + 1)
                pool.sem_inc(S["passed"], 1)
                for t in range(k0, k0 + tiles):
                    pool.indirect_dma_start(disp[phase], bass.IndirectOffsetOnAxis(ap=idx[:, t:t + 1], axis=0),
                                            XN[:, t, :], None).then_inc(S["scattered"], 16)

            def experts(phase):
                with pool.Fori(0, E // 2) as ee:
                    for u in range(2):
                        pool.wait_ge(S["y_ready"], E * phase + 2 * ee + u + 1)
                        pool.sem_inc(S["passed"], 1)
                        for j in range(3):
                            m = min(P, CAP - P * j)
                            pool.indirect_dma_start(ytok[phase], bass.IndirectOffsetOnAxis(ap=who[u][0:m, j:j + 1], axis=0),
                                                    Y[u][0:m, j, :], None).then_inc(y_sc[u], 16)

            for k, (t0, tiles) in enumerate(FIRST):
                inv_std(k, t0, tiles)
            pool.memset(bvf[:], 0.0).then_inc(S["bv_zero"], 1)
            pool.memset(bvs[:], 0.0).then_inc(S["bvs_zero"], 1)
            for u in range(2):
                pool.memset(Vh[u][:, :, :, HD:HD + 1], 1.0)
            pool.wait_ge(S["slots_empty"], 32)
            for k, (t0, tiles) in enumerate(FIRST):
                dispatch(k, 0, t0, tiles)
            pool.wait_ge(S["amax"], 1)
            pool.partition_all_reduce(am[:, 1:2], am[:, 0:1], P, ABSMAX).then_inc(S["amax_all"], 1)
            experts(0)

            def low(dst, src, hi, done):
                pool.tensor_tensor(dst, src, hi, ALU.subtract).then_inc(done, 1)

            def qk_low(i, u):
                pool.wait_ge(S["q_hi"], i + 1)
                low(Qn[u][:, 1, :], Tq[:], Qn[u][:, 0, :], S["q_lo"])
                pool.wait_ge(S["k_hi"], i + 1)
                low(Kn[u][:, 1, :], Tk[:], Kn[u][:, 0, :], S["k_lo"])

            def v_low(i, u):
                pool.wait_ge(S["v_hi"], i + 1)
                low(Vl[u][:], Tv[u][:].rearrange("p (t h d) -> p t h d", t=GT, h=2), Vh[u][:, :, :, 0:HD], S["v_lo"])

            def p_low(s, u):
                for h in range(2):
                    for c in POOL_CHUNKS[h]:
                        a, n, _ = CHUNKS[c]
                        pool.wait_ge(S["p_hi"], 6 * s + 3 * h + c + 1)
                        low(Pl[u][h][:, a:a + n], Pf[u][h][:, a:a + n], Ph[u][h][:, a:a + n], S["p_lo_p"])

            def step(b, r, project=True, score=True, between=None):
                i, u = NPAIR * b + r, r % 2
                if project:
                    qk_low(i, u)
                if between:
                    between()
                if score:
                    p_low(i - 1, 1 - u)
                    v_low(i - 1, 1 - u)

            def batch_inv_std(b):
                inv_std(NS + NG + b, 0, GT)

            def batch_dispatch(b):
                dispatch(NS + b, 1, 0, GT)

            inv_std(NS, 0, GT)
            inv_std(NS + 1, 0, GT)
            for r in range(NPAIR):
                step(0, r, score=r > 0)
                if r in X_STATS:
                    inv_std(NS + X_STATS[r], 0, GT)
            pool.wait_ge(S["slots_empty"], 64)
            for r in range(NPAIR):
                step(1, r)
                if r == 4:
                    batch_inv_std(0)
            with pool.Fori(2, NG) as b:
                for r in range(NPAIR):
                    step(b, r, between=(lambda: batch_dispatch(b - 2)) if r == 3 else None)
                    if r == 4:
                        batch_inv_std(b - 1)
            step(NG, 0, project=False)
            batch_dispatch(NG - 2)
            batch_inv_std(NG - 1)
            batch_dispatch(NG - 1)
            experts(1)

        @block.scalar
        def _(act):
            act.sem_inc(S["yt"], 1)
            act.dma_start(rows[B1_COL:B1_COL + 32, :], b1.rearrange("e (t p) -> (e t) p", p=P)).then_inc(S["rows_in"], 16)
            act.dma_start(rows[BQ_COL:BQ_COL + 8, :], bq.rearrange("(r p) -> r p", p=P)).then_inc(S["rows_in"], 16)
            act.dma_start(rows[BK_COL:BK_COL + 8, :], bk.rearrange("(r p) -> r p", p=P)).then_inc(S["rows_in"], 16)
            act.dma_start(rows[BO_COL:BO_COL + 1, :], bo.rearrange("(r p) -> r p", p=P)).then_inc(S["rows_in"], 16)
            act.dma_start(rows[GW_COL:GW_COL + 8, :], gate_w).then_inc(S["rows_in"], 16)
            act.dma_start(b2bc[:], b2.rearrange("e d -> (e d)").partition_broadcast(P)).then_inc(S["b2_in"], 16)
            act.wait_ge(S["rt_ps"], 1)
            act.activation(RT[:], pj0[:, 0:ROWS], ACT.Copy).then_inc(S["rt_ready"], 1)
            for k, w in enumerate((wq, wk, wv)):
                act.dma_start(Wf[:, 1024 * k:1024 * (k + 1)], w).then_inc(S["w_in"], 16)
            act.dma_start(Wf[:, 3072:4096].rearrange("p (r d) -> p r d", d=P), wo.rearrange("(r p) d -> p r d", p=P)).then_inc(S["w_in"], 16)

            def experts(phase):
                with act.Fori(0, E // 2) as ee:
                    for u in range(2):
                        for ft in range(FT):
                            k = FT * (2 * ee + u) + ft
                            act.wait_ge(S["h_ps"], FT * E * phase + k + 1)
                            act.activation(hT[u][:, ft, :], hbank[ft][:, 0:CAP], ACT.Relu,
                                           bias=RT[:, bass.ds(B1_COL + k, 1)]).then_inc(S["h_ready"], 1)

            def copy_xt(n, g, ps):
                act.wait_ge(S["xt_ps"], n + 1)
                act.activation(xT[:, GN * g:GN * g + GN], ps[:], ACT.Copy).then_inc(S["xt_ready"], 1)

            def exp_logits(n, k0, tiles):
                act.wait_ge(S["dl_ready"], n + 1)
                act.activation(el[:, k0:k0 + tiles], dl[:, k0:k0 + tiles], ACT.Exp).then_inc(S["el_ready"], 1)

            def split_x(g):
                act.wait_ge(S["xa_ps"], g + 1)
                act.activation(XH[:, GN * g:GN * g + GN], tT[:], ACT.Copy).then_inc(S["x_hi"], 1)

            copy_xt(0, 0, sc[0])
            copy_xt(1, 1, sc[1])
            exp_logits(0, *FIRST[0])
            copy_xt(2, 2, sc[0])
            copy_xt(3, 3, sc[1])
            exp_logits(1, *FIRST[1])
            exp_logits(2, *FIRST[2])
            for k in range(3):
                if k == 0:
                    act.wait_ge(S["bv_zero"], 1)
                act.dma_start(bvf[32 * k:32 * k + 1, :], bv.rearrange("(a n) -> a n", a=1)).then_inc(S["bv_in"], 16)
            experts(0)
            split_x(0)

            unscale = am[:, 5:6]

            def tanh_qk(i, r):
                first = isinstance(i, int) and i == 0
                act.wait_ge(S["q_ps"], i + 1)
                if not first:
                    act.wait_ge(S["q_lo"], i)
                act.activation(Tq[:], pj0[:], ACT.Tanh, bias=RT[:, BQ_COL + r:BQ_COL + r + 1], scale=unscale).then_inc(S["tq"], 1)
                act.wait_ge(S["k_ps"], i + 1)
                if not first:
                    act.wait_ge(S["k_lo"], i)
                act.activation(Tk[:], pj1[:], ACT.Tanh, bias=RT[:, BK_COL + r:BK_COL + r + 1], scale=unscale).then_inc(S["tk"], 1)
                act.wait_ge(S["tk"], i + 1)
                act.activation(Kn[r % 2][:, 0, :], Tk[:], ACT.Copy).then_inc(S["k_hi"], 1)

            def tanh_v(i, u):
                act.wait_ge(S["v_ps"], i + 1)
                if not (isinstance(i, int) and i < 2):
                    act.wait_ge(S["v_lo"], i - 1)
                act.activation(Tv[u][:], pj0[:], ACT.Tanh, scale=unscale).then_inc(S["tv"], 1)

            def v_high(i, u):
                act.wait_ge(S["tv"], i + 1)
                if not (isinstance(i, int) and i < 2):
                    act.wait_ge(S["ctx_ps"], 2 * i - 2)
                act.activation(Vh[u][:, :, :, 0:HD], Tv[u][:].rearrange("p (t h d) -> p t h d", t=GT, h=2),
                               ACT.Copy).then_inc(S["v_hi"], 1)

            def exps(s, u, h):
                for c, (a, n, _) in enumerate(CHUNKS):
                    act.wait_ge(S["s_ps"], 6 * s + 3 * h + c + 1)
                    if not (isinstance(s, int) and s < 2):
                        act.wait_ge(*low_part(s - 2, h, c))
                    act.activation(Pf[u][h][:, a:a + n], sc[c][:, 0:n], ACT.Exp, scale=0.125,
                                   bias=pshift[:]).then_inc(S["exp_done"], 1)

            def ct_high(t, r):
                act.wait_ge(S["ct_ps"], t + 1)
                act.activation(CT[:, r, 0, :], tT[:], ACT.Copy).then_inc(S["ct_hi"], 1)

            def out_tanh(b, ps):
                act.wait_ge(S["wo_ps"], b + 1)
                act.activation(yT[:], ps[:], ACT.Tanh, bias=RT[:, BO_COL:BO_COL + 1], scale=unscale).then_inc(S["yt"], 1)

            def step(b, r, project=True, score=True, turn=True, between=None):
                i, u = NPAIR * b + r, r % 2
                if project:
                    tanh_qk(i, r)
                if between:
                    between()
                if score:
                    exps(i - 1, 1 - u, 0)
                if project:
                    tanh_v(i, u)
                if score:
                    exps(i - 1, 1 - u, 1)
                if turn:
                    ct_high(i - 3, (r - 3) % NPAIR)
                if score:
                    v_high(i - 1, 1 - u)

            for r in range(NPAIR):
                step(0, r, score=r > 0, turn=r > 2, between=(lambda: split_x(X_TURN[r])) if r in X_TURN else None)
            with act.Fori(1, NG) as b:
                between = {3: lambda: out_tanh(b - 1, tT), 6: lambda: copy_xt(NG - 1 + b, 0, tT),
                           7: lambda: exp_logits(NS - 1 + b, 0, GT)}
                for r in range(NPAIR):
                    step(b, r, between=between.get(r))
            step(NG, 0, project=False)
            ct_high(NPAIR * NG - 2, NPAIR - 2)
            ct_high(NPAIR * NG - 1, NPAIR - 1)
            out_tanh(NG - 1, pj1)
            copy_xt(2 * NG - 1, 0, tT)
            exp_logits(NS - 1 + NG, 0, GT)
            experts(1)

        @block.tensor
        def _(pe):
            mm = nc.tensor.matmul

            def transpose_group(src, ps, done):
                for t in range(GT):
                    last = nc.tensor.transpose(ps[:, P * t:P * t + P], src[:, t, 0:P], identf[:])
                last.then_inc(done, 1)

            def logits(g, at, ps, done):
                for t in range(GT):
                    o = E * (GT * at + t)
                    last = mm(ps[:, o:o + E], xT[:, P * (GT * g + t):P * (GT * g + t) + P], RT[:, GW_COL:GW_COL + E],
                              start=True, stop=True)
                if done:
                    last.then_inc(S["logit_ps"], 1)

            def rank_tokens(n, k0, tiles, ps):
                pe.wait_ge(S["mask_ready"], n + 1)
                mm(ps[:, 0:tiles * E], lower[:], mask[:, k0:k0 + tiles, :].rearrange("p t e -> p (t e)"), start=True, stop=False)
                for t in range(tiles - 1):
                    mm(ps[:, E * (t + 1):tiles * E].rearrange("p (t e) -> p t e", e=E), onesb[:],
                       mask[:, k0 + t:k0 + t + 1, :].broadcast_to([P, tiles - 1 - t, E]), start=False, stop=t == tiles - 2)
                for t in range(tiles):
                    last = mm(ps[:, tiles * E:(tiles + 1) * E], onesb[:], mask[:, k0 + t, :], start=t == 0, stop=t == tiles - 1)
                last.then_inc(S["rank_ps"], 1)

            def experts(phase):
                def tokens(n, u, cnt):
                    pe.wait_ge(xe_in[u], 32 * (cnt + 1))
                    nc.tensor.transpose(tT[:, 0:P], XE[u][:, 0, 0:P], identf[:])
                    nc.tensor.transpose(tT[:, P:2 * P], XE[u][:, 1, 0:P], identf[:])
                    m = CAP - 2 * P
                    nc.tensor.transpose(tT[:, 2 * P:CAP], XE[u][0:m, 2, 0:P], identf[0:m, 0:m]).then_inc(S["xe_ps"], 1)

                def hidden(n, u, cnt, first=False):
                    pe.wait_ge(w1_in[u], 16 * (cnt + 1))
                    pe.wait_ge(S["xe_ready"], n + 1)
                    for ft in range(FT):
                        if not first:
                            pe.wait_ge(S["h_ready"], FT * (n - 1) + ft + 1)
                        mm(hbank[ft][:, 0:CAP], W1[u][:, P * ft:P * ft + P], xeT[:], start=True, stop=True).then_inc(S["h_ps"], 1)

                def outputs(n, u, cnt):
                    pe.wait_ge(w2_in[u], 16 * (cnt + 1))
                    ybank = (pj0, pj1)[u]
                    for j, m in enumerate((P, P, CAP - 2 * P)):
                        for ft in range(FT):
                            if j == 0:
                                pe.wait_ge(S["h_ready"], FT * n + ft + 1)
                            last = mm(ybank[0:m, P * j:P * j + P], hT[u][:, ft, P * j:P * j + m], W2[u][:, ft, :],
                                      start=ft == 0, stop=ft == FT - 1)
                    last.then_inc(S["y_ps"], 1)

                n0, c0 = E * phase, E // 2 * phase
                tokens(n0, 0, c0)
                hidden(n0, 0, c0, first=True)
                tokens(n0 + 1, 1, c0)
                with pe.Fori(0, E // 2 - 1) as ee:
                    for u in range(2):
                        n = n0 + 2 * ee + u
                        hidden(n + 1, 1 - u, c0 + ee + u)
                        tokens(n + 2, u, c0 + ee + 1)
                        outputs(n, u, c0 + ee)
                hidden(n0 + E - 1, 1, c0 + E // 2 - 1)
                outputs(n0 + E - 2, 0, c0 + E // 2 - 1)
                pe.wait_ge(S["y_ready"], n0 + E - 2)
                outputs(n0 + E - 1, 1, c0 + E // 2 - 1)

            pe.wait_ge(S["consts"], 1)
            pe.wait_ge(S["rows_in"], 80)
            nc.tensor.transpose(pj0[:, 0:ROWS], rows[:], identf[0:ROWS, 0:ROWS]).then_inc(S["rt_ps"], 1)
            pe.wait_ge(S["rt_ready"], 1)
            lbank, rbank = (pj0, cA, sc[2]), (pj1, cB, tT)

            def turn_first(g):
                pe.wait_ge(S["xn_ready"], g + 1)
                if g >= 2:
                    pe.wait_ge(S["xt_ready"], g - 1)
                transpose_group(XN[:, GT * g:GT * g + GT], sc[g % 2], S["xt_ps"])

            def first_logits(g, k):
                t0, tiles = FIRST[k]
                pe.wait_ge(S["xt_ready"], g + 1)
                logits(g, g - t0 // GT, lbank[k], GT * (g + 1) == t0 + tiles)

            turn_first(0)
            first_logits(0, 0)
            turn_first(1)
            first_logits(1, 1)
            rank_tokens(0, *FIRST[0], rbank[0])
            turn_first(2)
            turn_first(3)
            first_logits(2, 2)
            rank_tokens(1, *FIRST[1], rbank[1])
            first_logits(3, 2)
            rank_tokens(2, *FIRST[2], rbank[2])
            experts(0)

            def norm_x(g):
                pe.wait_ge(S["xa_ready"], g + 1)
                if g:
                    pe.wait_ge(S["x_lo"], g)
                transpose_group(xa, tT, S["xa_ps"])

            norm_x(0)

            def wpart(w, lowpart, r):
                return (WL if lowpart else WH)[:, 1024 * w + P * r:1024 * w + P * r + P]

            TERMS = ((0, 0), (1, 0), (0, 1))

            def qk(i, b, r):
                first = isinstance(i, int) and i == 0
                if r == 0:
                    pe.wait_ge(S["x_lo"], b + 1)
                if not first:
                    pe.wait_ge(S["tv"], i)
                for w, ps, done in ((0, pj0, "q_ps"), (1, pj1, "k_ps")):
                    if w and not first:
                        pe.wait_ge(S["tk"], i)
                    if w and r == 0 and not first:
                        pe.wait_ge(S["rank_read"], NS + b - 1)
                    for t, (wl, xl) in enumerate(TERMS):
                        last = mm(ps[:], wpart(w, wl, r), (XL if xl else XH)[:, bass.ds(GN * b, GN)],
                                  start=t == 0, stop=t == 2)
                    last.then_inc(S[done], 1)

            def v(i, b, r):
                pe.wait_ge(S["tq"], i + 1)
                for t in range(GT):
                    o = pj0[:, P * t:P * t + P]
                    for k, (wl, xl) in enumerate(TERMS):
                        mm(o, (XL if xl else XH)[:, bass.ds(GN * b + P * t, P)], wpart(2, wl, r), start=k == 0, stop=False)
                    last = mm(o, onesb[:], bvs[:, P * r:P * r + P], start=False, stop=True)
                last.then_inc(S["v_ps"], 1)

            def scores(s, u, cnt, between=None, sc2_read=None):
                pe.wait_ge(qs_in[u], 64 * (cnt + 1))
                pe.wait_ge(ks_in[u], 32 * (cnt + 1))
                pe.wait_ge(S["own_half"], s + 1)
                for h in range(2):
                    if h and between:
                        between()
                    for c, (a, n, kts) in enumerate(CHUNKS):
                        if h:
                            pe.wait_ge(S["exp_done"], 6 * s + c + 1)
                        elif not (isinstance(s, int) and s == 0):
                            pe.wait_ge(S["exp_done"], 6 * (s - 1) + 3 + c + 1)
                        if sc2_read and c == 2 and h == 0:
                            pe.wait_ge(*sc2_read)
                        for kt in kts:
                            o = KOFF[kt] - a
                            w = GN - P * kt
                            for part in range(2):
                                mm(sc[c][:, o:o + w], KS[u][h][:, part, P * kt:P * kt + P], QS[u][h][:, P * kt:GN],
                                   start=part == 0, stop=False)
                            last = mm(sc[c][:, o:o + P], identb[:], maskn[:], start=False, stop=True)
                        last.then_inc(S["s_ps"], 1)

            def context(c, u):
                pe.wait_ge(S["v_lo"], c + 1)
                for h in range(2):
                    pe.wait_ge(S["p_hi"], 6 * c + 3 * h + 3)
                    pe.wait_ge(*low_part(c, h, POOL_CHUNKS[h][-1]))
                    pe.wait_ge(*low_part(c, h, V_CHUNKS[h][-1]))
                    for qt in range(GT):
                        o = (HD + 1) * qt
                        for kt in range(qt + 1):
                            a = KOFF[kt] + P * (qt - kt)
                            mm(cx[h][:, o:o + HD + 1], Ph[u][h][:, a:a + P], Vh[u][:, kt, h, :], start=kt == 0, stop=False)
                            mm(cx[h][:, o:o + HD], Ph[u][h][:, a:a + P], Vl[u][:, kt, h, :], start=False, stop=False)
                            last = mm(cx[h][:, o:o + HD + 1], Pl[u][h][:, a:a + P], Vh[u][:, kt, h, :], start=False, stop=kt == qt)
                    last.then_inc(S["ctx_ps"], 1)

            def tt_free(t):
                pe.wait_ge(S["ct_lo"], t + 1)

            def context_t(t):
                pe.wait_ge(S["ctxn"], 2 * t + 2)
                tt_free(t)
                transpose_group(cn, tT, S["ct_ps"])

            def project_out(b, ps, first=0, end=NPAIR):
                tt_free(NPAIR * b + end)
                for r in range(first, end):
                    for t, (wl, cl) in enumerate(TERMS):
                        last = mm(ps[:], (WL if wl else WH)[:, 3072 + P * r:3072 + P * r + P], CT[:, r, cl, :],
                                  start=r == 0 and t == 0, stop=r == NPAIR - 1 and t == 2)
                if end == NPAIR:
                    last.then_inc(S["wo_ps"], 1)

            def turn_out(b):
                pe.wait_ge(S["yt"], b + 2)
                for t in range(GT):
                    last = nc.tensor.transpose(tT[:, P * t:P * t + P], yT[:, P * t:P * t + P], identf[:])
                last.then_inc(S["yt_ps"], 1)

            def turn_batch(b):
                pe.wait_ge(S["xn_ready"], NG + b + 1)
                transpose_group(XN, tT, S["xt_ps"])

            def route_logits(b, ps):
                pe.wait_ge(S["xt_ready"], NG + b + 1)
                logits(0, 0, ps, True)

            def rank_batch(b, ps):
                rank_tokens(NS + b, 0, GT, ps)

            def step(b, r, project=True, score=True, mix=True, turn=True, early=None, late=None, end=None,
                     sc2_read=None, tt_read=None):
                i, u = NPAIR * b + r, r % 2
                if project:
                    qk(i, b, r)
                if early:
                    if turn:
                        tt_free(i - 3)
                    early()
                if score:
                    scores(i - 1, 1 - u, NPAIR // 2 * b + (r - 1) // 2, (lambda: v(i, b, r)) if project else None, sc2_read)
                elif project:
                    v(i, b, r)
                if turn:
                    if tt_read:
                        pe.wait_ge(*tt_read)
                    context_t(i - 3)
                if late:
                    pe.wait_ge(S["tk"], i + 1)
                    late()
                if mix:
                    context(i - 2, u)
                if end:
                    pe.wait_ge(S["exp_done"], 6 * i)
                    end()

            pe.wait_ge(S["w_split"], E)
            pe.wait_ge(S["bv_ready"], 8)
            for r in range(NPAIR):
                turned = r in X_TURN
                step(0, r, score=r > 0, mix=r > 1, turn=r > 2, early=(lambda: norm_x(X_TURN[r])) if turned else None,
                     tt_read=(S["x_lo"], NG) if r == 3 else None)
            with pe.Fori(1, NG) as b:
                early = {3: lambda: project_out(b - 1, tT), 4: lambda: turn_out(b - 1), 6: lambda: turn_batch(b - 1)}
                tt_read = {3: (S["yt"], b + 1),
                           4: (S["x_added"], b),
                           6: (S["xt_ready"], NG + b)}
                late = {7: lambda: rank_batch(b - 1, pj1)}
                end = {6: lambda: route_logits(b - 1, sc[2])}
                sc2_read = {7: (S["dl_ready"], NS + b)}
                for r in range(NPAIR):
                    step(b, r, early=early.get(r), late=late.get(r), end=end.get(r),
                         sc2_read=sc2_read.get(r), tt_read=tt_read.get(r))
            pairs = NPAIR * NG
            scores(pairs - 1, 1, pairs // 2 - 1)
            context_t(pairs - 3)
            pe.wait_ge(S["rank_read"], NS + NG - 1)
            project_out(NG - 1, pj1, 0, 5)
            context(pairs - 2, 0)
            context_t(pairs - 2)
            context(pairs - 1, 1)
            project_out(NG - 1, pj1, 5, 7)
            context_t(pairs - 1)
            project_out(NG - 1, pj1, 7, 8)
            turn_out(NG - 1)
            pe.wait_ge(S["x_added"], NG)
            turn_batch(NG - 1)
            route_logits(NG - 1, sc[2])
            rank_batch(NG - 1, cB)
            experts(1)

        @block.vector
        def _(dve):
            dve.sem_inc(S["ct_lo"], 1)
            cnt = {"ln": 0}

            def ln_stats(n, first_tile, k0, tiles):
                s = Steps(dve, S["stat_step"], 2 * n, 2)
                dve.memset(spare[:], 0.0)
                for t in range(tiles):
                    last = dve.bn_stats(st[:, k0 + t, :], X[:, bass.ds(first_tile + t, 1), :].rearrange("p a d -> p (a d)"))
                s.done(last)
                dve.memset(spare[:], 0.0)
                for t in range(k0, k0 + tiles):
                    last = dve.bn_aggr(mv[:, t, :], st[:, t, :])
                s.done(last)
                a = slice(k0, k0 + tiles)
                dve.tensor_scalar(ve[:, a], mv[:, a, 1], EPS, None, ALU.add).then_inc(S["var_ready"], 1)
                s.end()

            def ln_scale(n, k0, tiles):
                s = Steps(dve, S["scale_step"], 3 * n, 3)
                dve.wait_ge(S["rs_pow"], n + 1)
                a = slice(k0, k0 + tiles)
                s.done(dve.tensor_tensor(ra[:, a], r0[:, a], r0[:, a], ALU.mult))
                s.done(dve.scalar_tensor_tensor(rb[:, a], ra[:, a], -0.5, ve[:, a], ALU.mult, ALU.mult))
                s.done(dve.scalar_tensor_tensor(rstd[:, a], rb[:, a], 1.5, r0[:, a], ALU.add, ALU.mult))
                s.end()

            def ln_apply(dst, first_tile, k0, tiles, done):
                for t in range(tiles):
                    xt = X[:, bass.ds(first_tile + t, 1), :].rearrange("p a d -> p (a d)")
                    last = dve.tensor_scalar(dst[:, t, 0:P], xt, mv[:, k0 + t, 0:1], rstd[:, k0 + t:k0 + t + 1],
                                             ALU.subtract, ALU.mult)
                last.then_inc(done, 1)

            def choose(s, n, k0, tiles, ps):
                a = slice(k0, k0 + tiles)
                lg = ps[:, 0:tiles * E].rearrange("p (t e) -> p t e", e=E)
                wide = lambda v: v[:, a].unsqueeze(2).broadcast_to([P, tiles, E])
                dve.wait_ge(S["logit_ps"], n + 1)
                s.done(dve.tensor_reduce(mx[:, a], lg, X_AXIS, ALU.max))
                dve.tensor_tensor(dl[:, a], lg, wide(mx), ALU.subtract).then_inc(S["dl_ready"], 1)
                dve.wait_ge(S["dl_ready"], n + 1)
                s.done(dve.tensor_scalar(m0[:, a], dl[:, a], 0.0, None, ALU.is_equal))
                s.done(dve.tensor_tensor(ms[:, a], m0[:, a], pick[:].unsqueeze(1).broadcast_to([P, tiles, E]), ALU.mult))
                s.done(dve.tensor_reduce(m2[:, a], ms[:, a], X_AXIS, ALU.max))
                dve.tensor_tensor(mask[:, a], ms[:, a], wide(m2), ALU.is_equal).then_inc(S["mask_ready"], 1)

            def place(s, n, first_tile, k0, tiles, ps):
                a = slice(k0, k0 + tiles)
                every = lambda v: v[:].unsqueeze(1).broadcast_to([P, tiles, E])
                tiles_at = bass.ds(first_tile, tiles)
                dve.wait_ge(S["mask_ready"], n + 1)
                dve.tensor_tensor(bases[:, a], every(ebase), mask[:, a], ALU.mult)
                dve.wait_ge(S["rank_ps"], n + 1)
                s.done(dve.tensor_tensor(pos[:, a], ps[:, 0:tiles * E].rearrange("p (t e) -> p t e", e=E), every(carry), ALU.add))
                dve.tensor_reduce(base[:, a], bases[:, a], X_AXIS, ALU.add)
                dve.tensor_tensor(carry[:], carry[:], ps[:, tiles * E:(tiles + 1) * E], ALU.add).then_inc(S["rank_read"], 1)
                s.done(dve.tensor_tensor(ranks[:, a], pos[:, a], mask[:, a], ALU.mult))
                s.done(dve.tensor_reduce(rank[:, a], ranks[:, a], X_AXIS, ALU.add))
                dve.tensor_scalar(keep[:, a], rank[:, a], float(CAP), None, ALU.is_le)
                s.done(dve.tensor_tensor(slot[:, a], rank[:, a], base[:, a], ALU.add))
                s.done(dve.tensor_tensor(sd[:, a], slot[:, a], tok[:, tiles_at], ALU.subtract))
                s.done(dve.tensor_tensor(sk[:, a], sd[:, a], keep[:, a], ALU.mult))
                dve.tensor_tensor(idx[:, a], sk[:, a], tok[:, tiles_at], ALU.add).then_inc(S["idx_ready"], 1)
                dve.wait_ge(S["el_ready"], n + 1)
                s.done(dve.tensor_reduce(se[:, a], el[:, a], X_AXIS, ALU.add))
                s.done(dve.reciprocal(pr[:, a], se[:, a]))
                s.done(dve.scalar_tensor_tensor(wts[:, tiles_at], pr[:, a], 0.5, keep[:, a], ALU.mult, ALU.mult))
                s.end()

            def experts(phase):
                m = CAP - 2 * P

                def tokens(n, u, cnt):
                    dve.wait_ge(xe_in[u], 32 * (cnt + 1))
                    dve.tensor_copy(nxt[u][:, 0:2], XE[u][:, 0:2, P:ROW].rearrange("p j a -> p (j a)").bitcast(U32))
                    dve.tensor_copy(nxt[u][0:m, 2:3], XE[u][0:m, 2, P:ROW].bitcast(U32))
                    dve.wait_ge(S["xe_ps"], n + 1)
                    dve.tensor_copy(xeT[:], tT[:, 0:CAP]).then_inc(S["xe_ready"], 1)

                def keep_numbers(n, u, cnt):
                    dve.wait_ge(S["xe_ready"], n + 1)
                    if not (isinstance(cnt, int) and cnt == 0):
                        dve.wait_ge(y_sc[u], 48 * cnt)
                    dve.tensor_copy(who[u][:, 0:2], nxt[u][:, 0:2])
                    dve.tensor_copy(who[u][0:m, 2:3], nxt[u][0:m, 2:3]).then_inc(S["kept"], 1)

                def outputs(n, e, u):
                    yb = (pj0, pj1)[u]
                    dve.wait_ge(S["y_ps"], n + 1)
                    bias = b2bc[:, bass.ds(P * e, P)]
                    dve.tensor_tensor(Y[u][:, 0:2, :], yb[:, 0:2 * P].rearrange("p (j d) -> p j d", j=2),
                                      bias.unsqueeze(1).broadcast_to([P, 2, P]), ALU.add)
                    dve.tensor_tensor(Y[u][0:m, 2, :], yb[0:m, 2 * P:3 * P], b2bc[0:m, bass.ds(P * e, P)],
                                      ALU.add).then_inc(S["y_ready"], 1)

                def split_weights(e):
                    part = bass.ds(512 * e, 512)
                    dve.tensor_scalar(WH[:, part], Wf[:, part], am[:, 4:5], None, ALU.mult).then_inc(S["w_ready"], 1)
                    dve.wait_ge(S["w_ready"], e + 1)
                    dve.scalar_tensor_tensor(WL[:, part], Wf[:, part], am[:, 4:5], WH[:, part], ALU.mult,
                                             ALU.subtract).then_inc(S["w_split"], 1)

                n0, c0 = E * phase, E // 2 * phase
                tokens(n0, 0, c0)
                tokens(n0 + 1, 1, c0)

                def pair(ee, last):
                    for u in range(2):
                        e = 2 * ee + u
                        keep_numbers(n0 + e, u, c0 + ee)
                        if not last:
                            dve.wait_ge(S["kept"], n0 + e + 1)
                            tokens(n0 + e + 2, u, c0 + ee + 1)
                        if phase == 0:
                            split_weights(e)
                        outputs(n0 + e, e, u)

                pair(0, False)
                with dve.Fori(1, E // 2 - 1) as ee:
                    pair(ee, False)
                pair(E // 2 - 1, True)

            def combine(phase, g):
                dve.wait_ge(gsem[g], 16 * (phase + 1))
                for t in range(GT * g, GT * g + GT):
                    last = dve.scalar_tensor_tensor(X[:, t, :], G[:, t, :], wts[:, t:t + 1], X[:, t, :], ALU.mult, ALU.add)
                last.then_inc(S["combined"], 1)

            dve.memset(carry[:], 0.0).then_inc(S["carry0"], 1)
            def first_stats(k):
                dve.wait_ge(x_in[k], 16)
                ln_stats(k, FIRST[k][0], *FIRST[k])

            def first_apply(k):
                t0, tiles = FIRST[k]
                ln_scale(k, t0, tiles)
                for t in range(t0, t0 + tiles, GT):
                    ln_apply(XN[:, t:t + GT], t, t, GT, S["xn_ready"])

            steps = [Steps(dve, S["route_step"], ROUTE_STEPS * k, ROUTE_STEPS) for k in range(NS)]

            def first_choose(k):
                choose(steps[k], k, *FIRST[k], (pj0, cA, sc[2])[k])

            def first_place(k):
                place(steps[k], k, FIRST[k][0], *FIRST[k], (pj1, cB, tT)[k])

            first_stats(0)
            first_stats(1)
            first_apply(0)
            first_stats(2)
            first_apply(1)
            dve.wait_ge(S["consts"], 2)
            dve.wait_ge(S["carry0"], 1)
            dve.tensor_copy(XN[:, :, P:ROW].rearrange("p t a -> p (t a)").bitcast(U32), number[:])
            first_choose(0)
            first_apply(2)
            first_place(0)
            first_choose(1)
            first_place(1)
            first_choose(2)
            first_place(2)
            dve.memset(carry[:], 0.0).then_inc(S["carry0"], 1)
            dve.wait_ge(S["w_in"], 64)
            s = Steps(dve, S["wscale"], 0, 8)
            s.done(dve.tensor_reduce(am[:, 0:1], Wf[:], X_AXIS, ALU.max))
            s.done(dve.tensor_reduce(am[:, 6:7], Wf[:], X_AXIS, ALU.min))
            s.done(dve.tensor_scalar(am[:, 7:8], am[:, 6:7], -1.0, None, ALU.mult))
            dve.tensor_tensor(am[:, 0:1], am[:, 0:1], am[:, 7:8], ALU.max).then_inc(S["amax"], 1)
            dve.wait_ge(S["amax_all"], 1)
            s.done(dve.tensor_scalar(am[:, 2:3], am[:, 1:2], 1e-30, None, ALU.max))
            s.done(dve.tensor_scalar(am[:, 3:4].bitcast(U32), am[:, 2:3].bitcast(U32), 0x7F800000, None, ALU.bitwise_and))
            s.done(dve.reciprocal(am[:, 6:7], am[:, 3:4]))
            s.done(dve.tensor_scalar(am[:, 4:5], am[:, 6:7], 2.0 ** 14, None, ALU.mult))
            s.done(dve.tensor_scalar(am[:, 5:6], am[:, 3:4], 2.0 ** -14, None, ALU.mult))
            s.end()
            dve.wait_ge(S["b2_in"], 16)
            experts(0)
            dve.wait_ge(S["bv_in"], 48)
            dve.wait_ge(S["bvs_zero"], 1)
            s = Steps(dve, S["bv_ready"], 0, 8)
            s.done(dve.tensor_scalar(bvr, bvf[:], am[:, 4:5], None, ALU.mult))
            s.done(dve.tensor_copy(bvt, bvr))
            s.done(dve.tensor_tensor(bvf[:], bvr, bvt, ALU.subtract))
            s.done(dve.tensor_copy(bvu, bvf[:]))
            s.done(dve.tensor_tensor(bvr, bvf[:], bvu, ALU.subtract))
            s.done(dve.tensor_copy(bvs[0:32, :], bvt[0:32, :]))
            s.done(dve.tensor_copy(bvs[32:64, :], bvu[32:64, :]))
            s.done(dve.tensor_copy(bvs[64:96, :], bvr[64:96, :]))
            s.end()

            def x_stats(g):
                combine(0, g)
                dve.wait_ge(S["combined"], g + 1)
                ln_stats(NS + g, GT * g, 0, GT)

            def x_apply(g):
                ln_scale(NS + g, 0, GT)
                if g:
                    dve.wait_ge(S["xa_ps"], g)
                ln_apply(xa, GT * g, 0, GT, S["xa_ready"])

            def x_low(g):
                dve.wait_ge(S["x_hi"], g + 1)
                dve.tensor_tensor(XL[:, GN * g:GN * g + GN], tT[:], XH[:, GN * g:GN * g + GN], ALU.subtract).then_inc(S["x_lo"], 1)

            x_stats(0)
            x_apply(0)
            x_low(0)
            x_stats(1)

            def q_high(i, u):
                dve.wait_ge(S["tq"], i + 1)
                dve.tensor_copy(Qn[u][:, 0, :], Tq[:]).then_inc(S["q_hi"], 1)

            def stack_k(i, u):
                dve.wait_ge(S["k_lo"], i + 1)
                for h in range(2):
                    last = dve.tensor_copy(KS[u][h][half(h)], Kn[u][half(h)])
                last.then_inc(S["own_half"], 1)

            late = []

            def make_low():
                k, u, h, a, n = late.pop()
                dve.wait_ge(S["p_hi"], k)
                dve.tensor_tensor(Pl[u][h][:, a:a + n], Pf[u][h][:, a:a + n], Ph[u][h][:, a:a + n],
                                  ALU.subtract).then_inc(S["p_lo_v"], 1)

            def split_p(s, u, h):
                for c, (a, n, _) in enumerate(CHUNKS):
                    k = 6 * s + 3 * h + c + 1
                    dve.wait_ge(S["exp_done"], k)
                    dve.tensor_copy(Ph[u][h][:, a:a + n], Pf[u][h][:, a:a + n]).then_inc(S["p_hi"], 1)
                    if late:
                        make_low()
                    if c in V_CHUNKS[h]:
                        late.append((k, u, h, a, n))
                if late:
                    make_low()

            def normalise(c):
                heads = [cx[h][:, 0:GT * (HD + 1)].rearrange("p (t d) -> p t d", d=HD + 1) for h in range(2)]
                for h in range(2):
                    dve.wait_ge(S["ctx_ps"], 2 * c + h + 1)
                    dve.reciprocal(rden[h][:], heads[h][:, :, HD]).then_inc(S["rden_ready"], 1)
                    dve.wait_ge(S["rden_ready"], 2 * c + h + 1)
                    dve.tensor_tensor(cn[:, :, HD * h:HD * h + HD], heads[h][:, :, 0:HD],
                                      rden[h][:].unsqueeze(2).broadcast_to([P, GT, HD]), ALU.mult).then_inc(S["ctxn"], 1)

            def ct_low(t, r):
                dve.wait_ge(S["ct_hi"], t + 1)
                dve.tensor_tensor(CT[:, r, 1, :], tT[:], CT[:, r, 0, :], ALU.subtract).then_inc(S["ct_lo"], 1)

            def step(b, r, project=True, score=True, turn=True, between=None, late=None):
                i, u = NPAIR * b + r, r % 2
                if turn:
                    normalise(i - 3)
                if project:
                    q_high(i, u)
                if between:
                    between()
                if score:
                    split_p(i - 1, 1 - u, 0)
                if project:
                    stack_k(i, u)
                if late:
                    late()
                if score:
                    split_p(i - 1, 1 - u, 1)
                if turn:
                    ct_low(i - 3, (r - 3) % NPAIR)

            def add_out(b):
                dve.wait_ge(S["yt_ps"], b + 1)
                xg = X[:, bass.ds(GT * b, GT), :]
                dve.tensor_tensor(xg, xg, tT[:].rearrange("p (t d) -> p t d", d=P), ALU.add).then_inc(S["x_added"], 1)
                dve.wait_ge(S["x_added"], b + 1)

            def norm_batch(n, g):
                ln_scale(NS + NG - 1 + n, 0, GT)
                dve.wait_ge(S["scattered"], 16 * (NT + GT * g))
                dve.tensor_copy(XN[:, 0:GT, P:ROW].rearrange("p t a -> p (t a)").bitcast(U32), number[:, bass.ds(GT * g, GT)])
                ln_apply(XN, GT * g, 0, GT, S["xn_ready"])

            for r in range(NPAIR):
                def between():
                    if r in X_TURN:
                        x_low(X_TURN[r])
                    if r in X_APPLY:
                        x_apply(X_APPLY[r])

                step(0, r, score=r > 0, turn=r > 2, between=between)
                if r in X_STATS:
                    x_stats(X_STATS[r])
            dve.wait_ge(S["carry0"], 2)

            def batch_stats(b):
                ln_stats(NS + NG + b, GT * b, 0, GT)

            def batch_place(b, s, ps):
                place(s, NS + b, GT * b, 0, GT, ps)

            with dve.Fori(1, NG) as b:
                for r in range(NPAIR):
                    if r == 7:
                        s = Steps(dve, S["route_step"], ROUTE_STEPS * (NS + b - 1), ROUTE_STEPS)
                    step(b, r, between={4: lambda: add_out(b - 1), 5: lambda: norm_batch(b, b - 1),
                                        7: lambda: choose(s, NS + b - 1, 0, GT, sc[2])}.get(r),
                         late=(lambda: batch_place(b - 1, s, pj1)) if r == 7 else None)
                    if r == 4:
                        batch_stats(b - 1)
            step(NG, 0, project=False)
            normalise(NPAIR * NG - 2)
            ct_low(NPAIR * NG - 2, NPAIR - 2)
            normalise(NPAIR * NG - 1)
            ct_low(NPAIR * NG - 1, NPAIR - 1)
            add_out(NG - 1)
            batch_stats(NG - 1)
            norm_batch(NG, NG - 1)
            s = Steps(dve, S["route_step"], ROUTE_STEPS * (NS + NG - 1), ROUTE_STEPS)
            choose(s, NS + NG - 1, 0, GT, sc[2])
            batch_place(NG - 1, s, cB)
            experts(1)
            for g in range(NG):
                combine(1, g)


_INS = ["L0_attn_states", "L0_attn_Wq", "L0_attn_bq", "L0_attn_Wk", "L0_attn_bk", "L0_attn_Wv", "L0_attn_bv",
        "L0_attn_Wo", "L0_attn_bo", "L0_ffn_gate_w", "L0_ffn_w1", "L0_ffn_b1", "L0_ffn_w2", "L0_ffn_b2"]


def kernel(**inputs):
    import concourse.bacc as bacc
    from concourse.bass_utils import run_bass_kernel_spmd

    nc = bacc.Bacc("TRN2", target_bir_lowering=False, num_devices=1)
    arrays, args = {}, []
    for name in _INS:
        a = np.ascontiguousarray(inputs[name])
        arrays[f"in_{name}"] = a
        args.append(nc.dram_tensor(f"in_{name}", a.shape, mybir.dt.from_np(a.dtype), kind="ExternalInput").ap())
    args.append(nc.dram_tensor("out", (4, 512, 128), F32, kind="ExternalOutput").ap())
    macaron(nc, *args)
    r = run_bass_kernel_spmd(nc, [arrays], core_ids=[0])
    return r.results[0]["out"]
```
